# Optimizing a Trainium2 kernel written in Bass

```python
import numpy as np
import jax
import jax.numpy as jnp

def _softmax(x, axis=-1):
    return jax.nn.softmax(x, axis=axis)

def _gelu(x):
    return jax.nn.gelu(x, approximate=True)

def _silu(x):
    return jax.nn.silu(x)

def _sigmoid(x):
    return jax.nn.sigmoid(x)

def _layernorm(x, axis=-1, eps=1e-05):
    m = jnp.mean(x, axis=axis, keepdims=True)
    v = jnp.var(x, axis=axis, keepdims=True)
    return (x - m) / jnp.sqrt(v + eps)

def _scatter_add(tgt, idx, src, axis=0):
    return tgt.at[idx].add(src)

def _segment_sum(src, seg, n):
    return jax.ops.segment_sum(src, seg, n)
kernel_name = 'mk_gnn_resnorm_d2_gnn_r8_6ac9ea'

def setup_inputs(seed: int=0):
    np.random.seed(seed)
    _w = jnp.asarray

    def _rec_inputs():
        import jax
        import jax.numpy as jnp
        _gk = jax.random.key(seed)
        x = -0.0004287 + 1 * jax.random.normal(jax.random.fold_in(_gk, 1), (3125, 160), jnp.float32)
        _s = jax.random.randint(jax.random.fold_in(_gk, 2), (50000,), 0, 3125, jnp.int32)
        _d = jax.random.randint(jax.random.fold_in(_gk, 3), (50000,), 0, 3125, jnp.int32)
        _loop = jnp.arange(3125, dtype=jnp.int32)
        src = jnp.concatenate([_s, _d, _loop])
        dst = jnp.concatenate([_d, _s, _loop])
        _o = jnp.argsort(dst, stable=True)
        src = src[_o]
        dst = dst[_o]
        edge_attr_10 = jax.random.uniform(jax.random.fold_in(_gk, 12), (103125, 10), jnp.float32, 0.0, 1)
        edge_attr_4 = 0.000452788 + 0.999756 * jax.random.normal(jax.random.fold_in(_gk, 13), (103125, 4), jnp.float32)
        edge_attr_8 = jax.random.uniform(jax.random.fold_in(_gk, 14), (103125, 8), jnp.float32, 0.0, 1)
        node_vec1 = jax.random.uniform(jax.random.fold_in(_gk, 16), (3125, 1), jnp.float32, 0.0, 1)
        return (x, src, dst, edge_attr_10, edge_attr_4, edge_attr_8, node_vec1)
    x, src, dst, edge_attr_10, edge_attr_4, edge_attr_8, node_vec1 = _rec_inputs()

    def _L0_gnn_setup():
        import jax, jax.numpy as jnp
        import numpy as np
        N = 3125
        E = 50000
        MUL_S, MUL_V = (64, 32)
        NB, NH = (8, 64)
        WNUM = 64 + 64 + 32 + 32 + 32
        AVG_NEI = 16.0
        EPS = 1e-05
        INV_SQRT3 = 1.0 / np.sqrt(3.0)
        INV_SQRT2 = 1.0 / np.sqrt(2.0)

        def _split(x):
            return (x[:, :MUL_S], x[:, MUL_S:].reshape(-1, MUL_V, 3))

        def _forward(node_hiddens, edge_sh, edge_attr, W1_0, W1_1, Wfc1, Wfc2, Wfc3, W2_0, W2_1, Wsc0, Wsc1, g0, g1, edge_src, edge_dst):
            s_in, v_in = _split(node_hiddens)
            sc_s = s_in @ Wsc0 / np.sqrt(MUL_S)
            sc_v = jnp.einsum('nuc,uv->nvc', v_in, Wsc1) / np.sqrt(MUL_V)
            s = s_in @ W1_0 / np.sqrt(MUL_S)
            v = jnp.einsum('nuc,uv->nvc', v_in, W1_1) / np.sqrt(MUL_V)
            h = jax.nn.silu(edge_attr @ Wfc1 / np.sqrt(NB))
            h = jax.nn.silu(h @ Wfc2 / np.sqrt(NH))
            w = h @ Wfc3 / np.sqrt(NH)
            w0, w1, w2 = (w[:, :64], w[:, 64:128], w[:, 128:160])
            w3, w4 = (w[:, 160:192], w[:, 192:224])
            sd = s[edge_dst]
            vd = v[edge_dst]
            sh0 = edge_sh[:, :1]
            sh1 = edge_sh[:, 1:4]
            m0 = w0 * sd * sh0
            m1 = w3 * jnp.sum(vd * sh1[:, None, :], -1) * INV_SQRT3
            mv0 = (w1 * sd)[:, :, None] * sh1[:, None, :]
            mv1 = w2[:, :, None] * vd * sh0[:, :, None]
            sh1b = jnp.broadcast_to(sh1[:, None, :], vd.shape)
            mv2 = w4[:, :, None] * jnp.cross(vd, sh1b) * INV_SQRT2
            mid_s = jnp.concatenate([m0, m1], -1)
            mid_v = jnp.concatenate([mv0, mv1, mv2], 1)
            ns = jax.ops.segment_sum(mid_s, edge_src, num_segments=N) / np.sqrt(AVG_NEI)
            nv = jax.ops.segment_sum(mid_v, edge_src, num_segments=N) / np.sqrt(AVG_NEI)
            out_s = ns @ W2_0 / np.sqrt(96) + sc_s
            out_v = jnp.einsum('nuc,uv->nvc', nv, W2_1) / np.sqrt(128) + sc_v
            rms_s = jnp.sqrt(jnp.mean(out_s ** 2, -1, keepdims=True) + EPS)
            out_s = out_s / rms_s * g0
            rms_v = jnp.sqrt(jnp.mean(jnp.sum(out_v ** 2, -1), -1) + EPS)
            out_v = out_v / rms_v[:, None, None] * g1[None, :, None]
            return jnp.concatenate([out_s, out_v.reshape(-1, 3 * MUL_V)], -1)
        key = jax.random.key(seed)
        ks = jax.random.split(key, 16)
        inp = {}
        inp['node_hiddens'] = jax.random.normal(ks[0], (N, MUL_S + 3 * MUL_V), jnp.float32)
        inp['edge_index'] = jax.random.randint(ks[1], (2, E), 0, N)
        inp['edge_sh'] = jax.random.normal(ks[2], (E, 4), jnp.float32)
        inp['edge_attr'] = jax.random.uniform(ks[3], (E, NB), jnp.float32)
        inp['W1_0'] = jax.random.normal(ks[4], (MUL_S, MUL_S), jnp.float32)
        inp['W1_1'] = jax.random.normal(ks[5], (MUL_V, MUL_V), jnp.float32)
        inp['Wfc1'] = jax.random.normal(ks[6], (NB, NH), jnp.float32)
        inp['Wfc2'] = jax.random.normal(ks[7], (NH, NH), jnp.float32)
        inp['Wfc3'] = jax.random.normal(ks[8], (NH, WNUM), jnp.float32)
        inp['W2_0'] = jax.random.normal(ks[9], (96, MUL_S), jnp.float32)
        inp['W2_1'] = jax.random.normal(ks[10], (128, MUL_V), jnp.float32)
        inp['Wsc0'] = jax.random.normal(ks[11], (MUL_S, MUL_S), jnp.float32)
        inp['Wsc1'] = jax.random.normal(ks[12], (MUL_V, MUL_V), jnp.float32)
        inp['g0'] = jnp.ones((MUL_S,), jnp.float32)
        inp['g1'] = jnp.ones((MUL_V,), jnp.float32)
        return inp
    _L0_gnn_all = _L0_gnn_setup()
    _L0_gnn_in = {k: v for k, v in _L0_gnn_all.items() if k in ('W1_0', 'W1_1', 'Wfc1', 'Wfc2', 'Wfc3', 'W2_0', 'W2_1', 'Wsc0', 'Wsc1', 'g0', 'g1')}
    del _L0_gnn_all

    def _L1_gnn_setup():
        import jax, jax.numpy as jnp
        import numpy as np
        N_NODES = 6250
        N_EDGES = 100000
        MUL0, MUL1 = (64, 32)
        N_BASIS, N_RADIAL = (10, 100)
        W_NUMEL = 192
        NUM_NEIGHBORS = 16.0
        INV_SQRT3 = np.float32(1.0 / np.sqrt(3.0))
        RELU_GAIN = np.float32(np.sqrt(2.0))
        FAN_L2 = np.float32(np.sqrt(MUL0 + MUL1))

        def _fctp_scalar_attr(x0, x1, a, W0, W1):
            o0 = x0 @ W0 * a * (1.0 / np.sqrt(W0.shape[0]))
            o1 = jnp.einsum('nud,uw->nwd', x1, W1) * a[..., None] * (1.0 / np.sqrt(W1.shape[0]))
            return (o0, o1)
        key = jax.random.key(seed)
        ks = jax.random.split(key, 16)
        return {'node_input': jax.random.normal(ks[0], (N_NODES, MUL0 + 3 * MUL1), jnp.float32), 'node_attr': jnp.ones((N_NODES, 1), jnp.float32), 'edge_attr': jax.random.normal(ks[1], (N_EDGES, 4), jnp.float32), 'edge_length_embedded': jax.random.uniform(ks[2], (N_EDGES, N_BASIS), dtype=jnp.float32), 'W_si0': jax.random.normal(ks[3], (MUL0, MUL0), jnp.float32), 'W_si1': jax.random.normal(ks[4], (MUL1, MUL1), jnp.float32), 'W_l1_0': jax.random.normal(ks[5], (MUL0, MUL0), jnp.float32), 'W_l1_1': jax.random.normal(ks[6], (MUL1, MUL1), jnp.float32), 'W_l2_00': jax.random.normal(ks[7], (MUL0, MUL0), jnp.float32), 'W_l2_10': jax.random.normal(ks[8], (MUL1, MUL0), jnp.float32), 'W_l2_01': jax.random.normal(ks[9], (MUL0, MUL1), jnp.float32), 'W_l2_11': jax.random.normal(ks[10], (MUL1, MUL1), jnp.float32), 'W_fc1': jax.random.normal(ks[11], (N_BASIS, N_RADIAL), jnp.float32), 'W_fc2': jax.random.normal(ks[12], (N_RADIAL, W_NUMEL), jnp.float32), 'edge_src': jax.random.randint(ks[13], (N_EDGES,), 0, N_NODES), 'edge_dst': jax.random.randint(ks[14], (N_EDGES,), 0, N_NODES)}
    _L1_gnn_all = _L1_gnn_setup()
    _L1_gnn_in = {k: v for k, v in _L1_gnn_all.items() if k in ('W_si0', 'W_si1', 'W_l1_0', 'W_l1_1', 'W_l2_00', 'W_l2_10', 'W_l2_01', 'W_l2_11', 'W_fc1', 'W_fc2')}
    del _L1_gnn_all
    return {'x': x, 'src': src, 'dst': dst, 'edge_attr_10': edge_attr_10, 'edge_attr_4': edge_attr_4, 'edge_attr_8': edge_attr_8, 'node_vec1': node_vec1, 'L0_gnn_W1_0': _L0_gnn_in['W1_0'], 'L0_gnn_W1_1': _L0_gnn_in['W1_1'], 'L0_gnn_Wfc1': _L0_gnn_in['Wfc1'], 'L0_gnn_Wfc2': _L0_gnn_in['Wfc2'], 'L0_gnn_Wfc3': _L0_gnn_in['Wfc3'], 'L0_gnn_W2_0': _L0_gnn_in['W2_0'], 'L0_gnn_W2_1': _L0_gnn_in['W2_1'], 'L0_gnn_Wsc0': _L0_gnn_in['Wsc0'], 'L0_gnn_Wsc1': _L0_gnn_in['Wsc1'], 'L0_gnn_g0': _L0_gnn_in['g0'], 'L0_gnn_g1': _L0_gnn_in['g1'], 'L1_gnn_W_si0': _L1_gnn_in['W_si0'], 'L1_gnn_W_si1': _L1_gnn_in['W_si1'], 'L1_gnn_W_l1_0': _L1_gnn_in['W_l1_0'], 'L1_gnn_W_l1_1': _L1_gnn_in['W_l1_1'], 'L1_gnn_W_l2_00': _L1_gnn_in['W_l2_00'], 'L1_gnn_W_l2_10': _L1_gnn_in['W_l2_10'], 'L1_gnn_W_l2_01': _L1_gnn_in['W_l2_01'], 'L1_gnn_W_l2_11': _L1_gnn_in['W_l2_11'], 'L1_gnn_W_fc1': _L1_gnn_in['W_fc1'], 'L1_gnn_W_fc2': _L1_gnn_in['W_fc2']}

def reference(x, src, dst, edge_attr_10, edge_attr_4, edge_attr_8, node_vec1, L0_gnn_W1_0, L0_gnn_W1_1, L0_gnn_Wfc1, L0_gnn_Wfc2, L0_gnn_Wfc3, L0_gnn_W2_0, L0_gnn_W2_1, L0_gnn_Wsc0, L0_gnn_Wsc1, L0_gnn_g0, L0_gnn_g1, L1_gnn_W_si0, L1_gnn_W_si1, L1_gnn_W_l1_0, L1_gnn_W_l1_1, L1_gnn_W_l2_00, L1_gnn_W_l2_10, L1_gnn_W_l2_01, L1_gnn_W_l2_11, L1_gnn_W_fc1, L1_gnn_W_fc2):
    import jax
    import jax.numpy as jnp

    def _L0_gnn_ref(node_hiddens, edge_index, edge_sh, edge_attr, W1_0, W1_1, Wfc1, Wfc2, Wfc3, W2_0, W2_1, Wsc0, Wsc1, g0, g1):
        import jax, jax.numpy as jnp
        import numpy as np
        N = 3125
        E = 50000
        MUL_S, MUL_V = (64, 32)
        NB, NH = (8, 64)
        WNUM = 64 + 64 + 32 + 32 + 32
        AVG_NEI = 16.0
        EPS = 1e-05
        INV_SQRT3 = 1.0 / np.sqrt(3.0)
        INV_SQRT2 = 1.0 / np.sqrt(2.0)

        def _split(x):
            return (x[:, :MUL_S], x[:, MUL_S:].reshape(-1, MUL_V, 3))

        def _forward(node_hiddens, edge_sh, edge_attr, W1_0, W1_1, Wfc1, Wfc2, Wfc3, W2_0, W2_1, Wsc0, Wsc1, g0, g1, edge_src, edge_dst):
            s_in, v_in = _split(node_hiddens)
            sc_s = s_in @ Wsc0 / np.sqrt(MUL_S)
            sc_v = jnp.einsum('nuc,uv->nvc', v_in, Wsc1) / np.sqrt(MUL_V)
            s = s_in @ W1_0 / np.sqrt(MUL_S)
            v = jnp.einsum('nuc,uv->nvc', v_in, W1_1) / np.sqrt(MUL_V)
            h = jax.nn.silu(edge_attr @ Wfc1 / np.sqrt(NB))
            h = jax.nn.silu(h @ Wfc2 / np.sqrt(NH))
            w = h @ Wfc3 / np.sqrt(NH)
            w0, w1, w2 = (w[:, :64], w[:, 64:128], w[:, 128:160])
            w3, w4 = (w[:, 160:192], w[:, 192:224])
            sd = s[edge_dst]
            vd = v[edge_dst]
            sh0 = edge_sh[:, :1]
            sh1 = edge_sh[:, 1:4]
            m0 = w0 * sd * sh0
            m1 = w3 * jnp.sum(vd * sh1[:, None, :], -1) * INV_SQRT3
            mv0 = (w1 * sd)[:, :, None] * sh1[:, None, :]
            mv1 = w2[:, :, None] * vd * sh0[:, :, None]
            sh1b = jnp.broadcast_to(sh1[:, None, :], vd.shape)
            mv2 = w4[:, :, None] * jnp.cross(vd, sh1b) * INV_SQRT2
            mid_s = jnp.concatenate([m0, m1], -1)
            mid_v = jnp.concatenate([mv0, mv1, mv2], 1)
            ns = jax.ops.segment_sum(mid_s, edge_src, num_segments=N) / np.sqrt(AVG_NEI)
            nv = jax.ops.segment_sum(mid_v, edge_src, num_segments=N) / np.sqrt(AVG_NEI)
            out_s = ns @ W2_0 / np.sqrt(96) + sc_s
            out_v = jnp.einsum('nuc,uv->nvc', nv, W2_1) / np.sqrt(128) + sc_v
            rms_s = jnp.sqrt(jnp.mean(out_s ** 2, -1, keepdims=True) + EPS)
            out_s = out_s / rms_s * g0
            rms_v = jnp.sqrt(jnp.mean(jnp.sum(out_v ** 2, -1), -1) + EPS)
            out_v = out_v / rms_v[:, None, None] * g1[None, :, None]
            return jnp.concatenate([out_s, out_v.reshape(-1, 3 * MUL_V)], -1)
        edge_src = edge_index[0]
        edge_dst = edge_index[1]
        return _forward(node_hiddens, edge_sh, edge_attr, W1_0, W1_1, Wfc1, Wfc2, Wfc3, W2_0, W2_1, Wsc0, Wsc1, g0, g1, edge_src, edge_dst)

    def _L1_gnn_ref(node_input, node_attr, edge_src, edge_dst, edge_attr, edge_length_embedded, W_si0, W_si1, W_l1_0, W_l1_1, W_l2_00, W_l2_10, W_l2_01, W_l2_11, W_fc1, W_fc2):
        import jax, jax.numpy as jnp
        import numpy as np
        N_NODES = 6250
        N_EDGES = 100000
        MUL0, MUL1 = (64, 32)
        N_BASIS, N_RADIAL = (10, 100)
        W_NUMEL = 192
        NUM_NEIGHBORS = 16.0
        INV_SQRT3 = np.float32(1.0 / np.sqrt(3.0))
        RELU_GAIN = np.float32(np.sqrt(2.0))
        FAN_L2 = np.float32(np.sqrt(MUL0 + MUL1))

        def _fctp_scalar_attr(x0, x1, a, W0, W1):
            o0 = x0 @ W0 * a * (1.0 / np.sqrt(W0.shape[0]))
            o1 = jnp.einsum('nud,uw->nwd', x1, W1) * a[..., None] * (1.0 / np.sqrt(W1.shape[0]))
            return (o0, o1)
        N = node_input.shape[0]
        x0 = node_input[:, :MUL0]
        x1 = node_input[:, MUL0:].reshape(N, MUL1, 3)
        a = node_attr
        h = jax.nn.relu(edge_length_embedded @ W_fc1 * (1.0 / np.sqrt(N_BASIS))) * RELU_GAIN
        w = h @ W_fc2 * (1.0 / np.sqrt(N_RADIAL))
        w0, w1, w2, w3 = (w[:, :64], w[:, 64:128], w[:, 128:160], w[:, 160:192])
        si0, si1 = _fctp_scalar_attr(x0, x1, a, W_si0, W_si1)
        l0, l1 = _fctp_scalar_attr(x0, x1, a, W_l1_0, W_l1_1)
        y0 = l0[edge_src]
        y1 = l1[edge_src]
        e0 = edge_attr[:, :1]
        e1 = edge_attr[:, 1:4]
        m0 = w0 * y0 * e0
        m1 = (w1 * y0)[:, :, None] * e1[:, None, :]
        m2 = (w2 * e0)[:, :, None] * y1
        m3 = w3 * jnp.einsum('eud,ed->eu', y1, e1) * INV_SQRT3
        inv = np.float32(1.0 / np.sqrt(NUM_NEIGHBORS))
        s0 = jax.ops.segment_sum(m0, edge_dst, num_segments=N) * inv
        s1 = jax.ops.segment_sum(m1, edge_dst, num_segments=N) * inv
        s2 = jax.ops.segment_sum(m2, edge_dst, num_segments=N) * inv
        s3 = jax.ops.segment_sum(m3, edge_dst, num_segments=N) * inv
        o0 = (s0 @ W_l2_00 + s3 @ W_l2_10) * a / FAN_L2
        o1 = (jnp.einsum('nud,uw->nwd', s1, W_l2_01) + jnp.einsum('nud,uw->nwd', s2, W_l2_11)) * a[..., None] / FAN_L2
        out0 = si0 + 0.5 * o0
        out1 = si1 + 0.5 * o1
        return jnp.concatenate([out0, out1.reshape(N, 3 * MUL1)], axis=1)
    edge_index = jnp.stack([src, dst])
    x = _layernorm(x + _L0_gnn_ref(x, edge_index, edge_attr_4, edge_attr_8, L0_gnn_W1_0, L0_gnn_W1_1, L0_gnn_Wfc1, L0_gnn_Wfc2, L0_gnn_Wfc3, L0_gnn_W2_0, L0_gnn_W2_1, L0_gnn_Wsc0, L0_gnn_Wsc1, L0_gnn_g0, L0_gnn_g1), axis=-1)
    x = _layernorm(x + _L1_gnn_ref(x, node_vec1, src, dst, edge_attr_4, edge_attr_10, L1_gnn_W_si0, L1_gnn_W_si1, L1_gnn_W_l1_0, L1_gnn_W_l1_1, L1_gnn_W_l2_00, L1_gnn_W_l2_10, L1_gnn_W_l2_01, L1_gnn_W_l2_11, L1_gnn_W_fc1, L1_gnn_W_fc2), axis=-1)
    return x

_drawn_inputs = setup_inputs


def setup_inputs(seed=0):
    import zlib

    import numpy as np

    out = dict(_drawn_inputs(seed))
    spreads = {'L0_gnn_g0': (1.0, 0.2), 'L0_gnn_g1': (1.0, 0.2)}
    factors = {}
    for name, (base, spread) in spreads.items():
        noise = np.random.default_rng([zlib.crc32(name.encode()), seed]).standard_normal(out[name].shape)
        drawn = base * np.exp(spread * noise) if base else spread * noise
        out[name] = jnp.asarray(drawn.astype(out[name].dtype))
    for name, factor in factors.items():
        out[name] = (out[name] * factor).astype(out[name].dtype)
    return out
```

```python
from contextlib import ExitStack

import numpy as np

import concourse.bass as bass
import concourse.mybir as mybir
from concourse.alu_op_type import AluOpType as ALU

F32 = mybir.dt.float32
I32 = mybir.dt.int32
ACT = mybir.ActivationFunctionType
AX = mybir.AxisListType

P = 128
N_NODES = 3125
N_EDGES = 103125
MUL_S, MUL_V = 64, 32
D_VEC = 3 * MUL_V
D = MUL_S + D_VEC
TILES = -(-N_NODES // P)
NODES_PAD = TILES * P
GROUP = 5
PAIR = 2
STEP = PAIR * P
RING = 4
ROUNDS = -(-N_EDGES // (STEP * RING))
STEPS = ROUNDS * RING
EDGES_PAD = STEPS * STEP
NB0, NB1 = 8, 10
REC = NB0 + NB1 + 4
SH = NB0 + NB1
NH0, NH1 = 64, 100
COPIES = 4
ACC_ROWS = NODES_PAD + P
EPS = 1e-5
BANK = 512
AVG = 0.25


def build(nc, t_in, out):
    ctx = ExitStack()
    with ctx:
        def sb(name, shape, dt=F32):
            return ctx.enter_context(nc.sbuf_tensor(name, shape, dt))

        def sem(name):
            return ctx.enter_context(nc.semaphore(name))

        psum = ctx.enter_context(nc.psum_tensor("psum", [P, 8, BANK], F32))
        X = sb("X", [P, TILES, D])
        skip = sb("skip", [P, TILES, D])
        sums = sb("sums", [P, COPIES, TILES, D])
        stage = sb("stage", [P, GROUP, D])
        xTs = sb("xTs", [MUL_S, GROUP, P])
        xTv = sb("xTv", [D_VEC, GROUP, P])
        table_rows = sb("table_rows", [P, GROUP, D])
        stat = sb("stat", [P, 6, TILES])
        ident = sb("ident", [P, P])
        before_mask = sb("before_mask", [P, P])
        dump_row = sb("dump_row", [P, 1])
        dump_row_i = sb("dump_row_i", [P, 1], I32)
        node_vec = sb("node_vec", [P, TILES])
        gains = sb("gains", [P, D - 2 * MUL_V])
        rec = sb("rec", [P, RING, PAIR, REC])
        key = sb("key", [P, RING, PAIR, 2], I32)
        target = sb("target", [P, RING, PAIR])
        gath = sb("gath", [P, RING, PAIR, D])
        recT = sb("recT", [PAIR * REC, 2, P])
        hidA = sb("hidA", [P, 2, PAIR * P])
        hidB = sb("hidB", [P, 2, P])
        outer = sb("outer", [P, PAIR, 3 * 192])
        sw = sb("sw", [P, PAIR, MUL_S])
        mid = sb("mid", [P, 2, PAIR, 480])
        midT = sb("midT", [P, PAIR, 4, P])
        same = sb("same", [P, RING, PAIR, P])
        junk = sb("junk", [P, PAIR, P])
        before = sb("before", [P, RING, PAIR])
        dump = sb("dump", [P, RING, PAIR])
        dest = sb("dest", [P, RING, PAIR], I32)
        msg = sb("msg", [P, PAIR, D])
        msg_sum = sb("msg_sum", [P, 2, PAIR, D])
        w = {k: sb("w_" + k, list(t_in[k].shape)) for k in WEIGHTS}

        table = [nc.dram_tensor(f"table{n}", [NODES_PAD, D], F32, kind="Internal").ap() for n in range(2)]
        acc = [[nc.dram_tensor(f"acc{n}_{c}", [ACC_ROWS, D], F32, kind="Internal").ap() for c in range(COPIES)]
               for n in range(2)]

        loaded, zeroed = sem("loaded"), sem("zeroed")
        const, scaled = sem("const"), sem("scaled")
        with nc.Block() as block:
            @block.sync
            def _(sp):
                sp.dma_start(X[:, :, :], t_in["x"].rearrange("(t p) d -> p t d", p=P)).then_inc(loaded, 16)
                sp.dma_start(node_vec[:, :], t_in["node_vec"]).then_inc(loaded, 16)
                sp.dma_start(gains[:, :], t_in["gains"].unsqueeze(0).broadcast_to([P, MUL_S + MUL_V])).then_inc(loaded, 16)
                for k in WEIGHTS:
                    sp.dma_start(w[k][:, :], t_in[k]).then_inc(loaded, 16)
                sp.wait_ge(loaded, 16 * (3 + len(WEIGHTS)))

            @block.gpsimd
            def _(pool):
                pool.memset(ident[:, :], 0.0).then_inc(const, 1)
                pool.memset(before_mask[:, :], 1.0).then_inc(const, 1)
                pool.iota(dump_row_i[:, :], pattern=[[0, 1]], base=NODES_PAD, channel_multiplier=1).then_inc(const, 1)
                pool.wait_ge(const, 3)
                pool.affine_select(out=ident[:, :], in_=ident[:, :], compare_op=ALU.not_equal, fill=1.0, base=0,
                                   pattern=[[-1, P]], channel_multiplier=1).then_inc(const, 1)
                pool.affine_select(out=before_mask[:, :], in_=before_mask[:, :], compare_op=ALU.is_gt, fill=0.0,
                                   base=0, pattern=[[-1, P]], channel_multiplier=1).then_inc(const, 1)

            @block.vector
            def _(dve):
                dve.wait_ge(const, 5)
                dve.tensor_copy(dump_row[:, :], dump_row_i[:, :]).then_inc(const, 1)
                dve.memset(sums[:, 0, :, :], 0.0).then_inc(scaled, 1)
                dve.memset(sums[:, 1, 0, :], 0.0).then_inc(scaled, 1)
                dve.wait_ge(loaded, 16 * (3 + len(WEIGHTS)))
                for k, lo, hi, f in SCALES:
                    dve.tensor_scalar(w[k][lo:hi, :], w[k][lo:hi, :], f, None, ALU.mult).then_inc(scaled, 1)

            @block.scalar
            def _(act):
                act.wait_ge(scaled, 2)
                for n in range(2):
                    for c in range(COPIES):
                        act.dma_start(acc[n][c].rearrange("(p r) d -> p (r d)", p=P),
                                      sums[:, 0:2, :, :].rearrange("p c t d -> p (c t d)")[:, 0:ACC_ROWS // P * D],
                                      ).then_inc(zeroed, 16)
                act.wait_ge(zeroed, 16 * 2 * COPIES)

        for layer in range(2):
            node_projection(nc, layer, sem, psum, X, skip, stage, xTs, xTv, table_rows, ident, node_vec, w,
                            table[layer])
            edge_layer(nc, layer, sem, psum, t_in, rec, key, target, gath, recT, hidA, hidB, outer, sw, mid, midT,
                       same, junk, before, dump, dest, msg, msg_sum, before_mask, dump_row, ident, w,
                       table[layer], acc[layer])
            finish_layer(nc, layer, sem, X, skip, sums, stat, gains, node_vec, acc[layer], out)


def node_projection(nc, layer, sem, psum, X, skip, stage, xTs, xTv, table_rows, ident, node_vec, w, table):
    flat = psum[:, :, :].rearrange("p b c -> p (b c)")
    staged, turned, taken = sem(f"n{layer}_staged"), sem(f"n{layer}_turned"), sem(f"n{layer}_taken")
    projected, evacuated, stored = sem(f"n{layer}_projected"), sem(f"n{layer}_evacuated"), sem(f"n{layer}_stored")
    OUT = 3
    results = psum[:, OUT:OUT + GROUP, :]
    table_v = table.rearrange("(t p) d -> p t d", p=P)
    groups = TILES // GROUP
    per_group = 3

    with nc.Block() as block:
        @block.vector
        def _(dve):
            with dve.Fori(0, groups) as g:
                dve.wait_ge(turned, g)
                dve.tensor_copy(stage[:, :, :], X[:, bass.ds(g * GROUP, GROUP), :]).then_inc(staged, 1)
                dve.wait_ge(turned, g + 1)
                dve.tensor_copy(xTv[:, :, :].rearrange("k t n -> k (t n)"),
                                flat[0:D_VEC, 2 * BANK:2 * BANK + GROUP * P]).then_inc(taken, 1)
                dve.wait_ge(projected, g + 1)
                if layer == 0:
                    dve.wait_ge(evacuated, g * per_group + 2)
                dve.tensor_copy(skip[:, bass.ds(g * GROUP, GROUP), :], results[:, :, D:2 * D]).then_inc(evacuated, 1)
                if layer == 1:
                    a = node_vec[:, bass.ds(g * GROUP, GROUP)].unsqueeze(2).broadcast_to([P, GROUP, D])
                    dve.wait_ge(stored, 16 * g)
                    dve.tensor_tensor(table_rows[:, :, :], results[:, :, 0:D], a, ALU.mult).then_inc(evacuated, 2)

        @block.tensor
        def _(pe):
            with pe.Fori(0, groups) as g:
                pe.wait_ge(staged, g + 1)
                pe.wait_ge(evacuated, g * per_group)
                for k in range(GROUP):
                    pe.transpose(flat[0:D_VEC, 2 * BANK + k * P:2 * BANK + (k + 1) * P], stage[:, k, MUL_S:D], ident[:, :])
                    mm = pe.transpose(flat[0:MUL_S, k * P:(k + 1) * P], stage[:, k, 0:MUL_S], ident[:, :])
                mm.then_inc(turned, 1)
                pe.wait_ge(taken, 2 * g + 2)
                for k in range(GROUP):
                    for half in range(2):
                        ws = w[f"node_s{layer}"][:, half * MUL_S:(half + 1) * MUL_S]
                        wv = w[f"node_v{layer}"][:, half * D_VEC:(half + 1) * D_VEC]
                        pe.matmul(psum[:, OUT + k, half * D:half * D + MUL_S], xTs[:, k, :], ws, start=True, stop=True)
                        mm = pe.matmul(psum[:, OUT + k, half * D + MUL_S:(half + 1) * D], xTv[:, k, :], wv,
                                       start=True, stop=True)
                mm.then_inc(projected, 1)

        @block.scalar
        def _(act):
            with act.Fori(0, groups) as g:
                act.wait_ge(turned, g + 1)
                act.activation(xTs[:, :, :].rearrange("k t n -> k (t n)"), flat[0:MUL_S, 0:GROUP * P],
                               ACT.Copy).then_inc(taken, 1)
                if layer == 0:
                    act.wait_ge(projected, g + 1)
                    act.wait_ge(stored, 16 * g)
                    act.activation(table_rows[:, :, :], results[:, :, 0:D], ACT.Copy).then_inc(evacuated, 2)

        @block.sync
        def _(sp):
            with sp.Fori(0, groups) as g:
                sp.wait_ge(evacuated, g * per_group + per_group)
                sp.dma_start(table_v[:, bass.ds(g * GROUP, GROUP), :], table_rows[:, :, :]).then_inc(stored, 16)
            sp.wait_ge(stored, 16 * groups)


def edge_layer(nc, layer, sem, psum, t_in, rec, key, target, gath, recT, hidA, hidB, outer, sw, mid, midT,
               same, junk, before, dump, dest, msg, msg_sum, before_mask, dump_row, ident, w, table, acc):
    L0 = layer == 0
    gather_col, scatter_col = (1, 0) if L0 else (0, 1)
    hidden = NH0 if L0 else NH1
    n_w = 224 if L0 else 192
    widths = [96, 128, 128, 128] if L0 else [96] * 4
    n_mid = sum(widths)
    starts = [sum(widths[:k]) for k in range(4)]
    out_s, out_v = w[f"out_s{layer}"], w[f"out_v{layer}"]
    mlp_in, mlp_out = w[f"mlp_in{layer}"], w[f"mlp_out{layer}"]
    rows_v = t_in["rec"].rearrange("(s p j) f -> s p (j f)", p=P, j=PAIR)
    keys_v = t_in["keys"].rearrange("(s p j) f -> s p (j f)", p=P, j=PAIR)

    def name(what):
        return sem(f"e{layer}_{what}")

    edges_loaded = [name(f"edges_loaded{u}") for u in range(RING)]
    gathered = [name(f"gathered{u}") for u in range(RING)]
    scattered = [name(f"scattered{c}") for c in range(COPIES)]
    target_ready, turned, recT_ready = name("target_ready"), name("turned"), name("recT_ready")
    hA_ready, actA_ready, hB_ready, actB_ready = name("hA"), name("actA"), name("hB"), name("actB")
    w_ready, mid_ready, midT_psum, midT_ready = name("w"), name("mid"), name("midT_psum"), name("midT")
    msg_psum, msg_ready, sum_psum, sum_ready = name("msg_psum"), name("msg"), name("sum_psum"), name("sum")
    same_ready, before_ready, dump_ready, dest_ready = name("same"), name("before"), name("dump"), name("dest")
    part = name("part")
    pool_turns = name("pool_turns")

    ps_turn = psum[:, 0, :]
    ps_hA = psum[:, 1, 0:PAIR * P]
    ps_hB = psum[:, 1, PAIR * P:PAIR * P + P]
    ps_w = [psum[:, 2 + b, 0:PAIR * n_w].rearrange("p (j n) -> p j n", j=PAIR) for b in range(2)]
    ps_mid = [psum[:, 4 + j, :].rearrange("p (k e) -> p k e", k=4) for j in range(PAIR)]
    ps_msg = psum[:, 6, 0:PAIR * D].rearrange("p (j d) -> p j d", j=PAIR)
    ps_sum = psum[:, 7, 0:PAIR * D].rearrange("p (j d) -> p j d", j=PAIR)

    def ahead(r, u, k):
        return r + (u + k) // RING, (u + k) % RING

    def exists(r, u):
        return not isinstance(r, int) or 0 <= RING * r + u < STEPS

    def not_first(r, u, depth):
        return not isinstance(r, int) or RING * r + u >= depth

    def run(eng, turn):
        for r in (-1, 0):
            for u in range(RING):
                turn(r, u)
        with eng.Fori(1, ROUNDS - 1) as r:
            for u in range(RING):
                turn(r, u)
        for u in range(RING):
            turn(ROUNDS - 1, u)

    def scalars(b):
        return mid[:, b, :, 0:96]

    def vectors(b):
        return mid[:, b, :, 96:n_mid].rearrange("p j (c n) -> p j c n", c=3)

    with nc.Block() as block:
        @block.sync
        def _(sp):
            def load(r, u):
                s = RING * r + u
                if not_first(r, u, RING):
                    sp.wait_ge(mid_ready, s - RING + 1)
                sp.dma_start(rec[:, u, :, :].rearrange("p j f -> p (j f)"),
                             rows_v[bass.ds(s, 1), :, :].rearrange("s p f -> (s p) f")).then_inc(edges_loaded[u], 16)
                sp.dma_start(key[:, u, :, :].rearrange("p j f -> p (j f)"),
                             keys_v[bass.ds(s, 1), :, :].rearrange("s p f -> (s p) f")).then_inc(edges_loaded[u], 16)
            for u in range(RING):
                load(0, u)
            with sp.Fori(1, ROUNDS) as r:
                for u in range(RING):
                    load(r, u)

        @block.gpsimd
        def _(pool):
            def gather(r, u):
                s = RING * r + u
                pool.wait_ge(edges_loaded[u], 32 * r + 32)
                if not_first(r, u, RING):
                    pool.wait_ge(mid_ready, s - RING + 1)
                pool.sem_inc(pool_turns, 1)
                for j in range(PAIR):
                    pool.indirect_dma_start(
                        gath[:, u, j, :], None, table,
                        bass.IndirectOffsetOnAxis(ap=key[:, u, j, gather_col:gather_col + 1], axis=0),
                    ).then_inc(gathered[u], 16)

            def scatter(r, u):
                s = RING * r + u
                pool.wait_ge(sum_ready, s + 1)
                pool.wait_ge(dest_ready, s + 1)
                for j in range(PAIR):
                    c = PAIR * (u % 2) + j
                    if not_first(r, u, 2):
                        pool.wait_ge(scattered[c], 32 * r + 16 * (u // 2))
                pool.sem_inc(pool_turns, 1)
                for j in range(PAIR):
                    c = PAIR * (u % 2) + j
                    pool.indirect_dma_start(
                        acc[c], bass.IndirectOffsetOnAxis(ap=dest[:, u, j:j + 1], axis=0),
                        msg_sum[:, u % 2, j, :], None, compute_op=ALU.add,
                    ).then_inc(scattered[c], 16)

            def turn(r, u):
                if exists(*ahead(r, u, 3)):
                    gather(*ahead(r, u, 3))
                if exists(r, u):
                    scatter(r, u)
            run(pool, turn)
            for c in range(COPIES):
                pool.wait_ge(scattered[c], 16 * STEPS // 2)

        @block.tensor
        def _(pe):
            def turn_edges(r, u):
                s = RING * r + u
                pe.wait_ge(edges_loaded[u], 32 * r + 32)
                if not_first(r, u, 1):
                    pe.wait_ge(same_ready, s)
                pe.wait_ge(target_ready, s + 1)
                for j in range(PAIR):
                    pe.transpose(ps_turn[:, P * (1 + j):P * (2 + j)], target[:, u, j:j + 1].broadcast_to([P, P]),
                                 ident[:, :])
                mm = pe.transpose(ps_turn[0:PAIR * REC, 0:P], rec[:, u, :, :].rearrange("p j f -> p (j f)"), ident[:, :])
                mm.then_inc(turned, 1)

            def hidden_a(r, u):
                s = RING * r + u
                if not_first(r, u, 1):
                    pe.wait_ge(actB_ready if L0 else actA_ready, s)
                pe.wait_ge(recT_ready, s + 1)
                if L0:
                    mm = pe.matmul(ps_hA[:, 0:P], mlp_in[:, :], recT[:, u % 2, :], start=True, stop=True)
                else:
                    for j in range(PAIR):
                        mm = pe.matmul(ps_hA[0:NH1, j * P:(j + 1) * P], mlp_in[:, j * NH1:(j + 1) * NH1],
                                       recT[:, u % 2, :], start=True, stop=True)
                mm.then_inc(hA_ready, 1)

            def hidden_b(r, u):
                s = RING * r + u
                pe.wait_ge(actA_ready, s + 1)
                pe.matmul(ps_hB, w["mlp_mid0"][:, :], hidA[:, u % 2, 0:P], start=True, stop=True).then_inc(hB_ready, 1)

            def edge_weights(r, u):
                s = RING * r + u
                if not_first(r, u, 2):
                    pe.wait_ge(mid_ready, s - 1)
                pe.wait_ge(actB_ready if L0 else actA_ready, s + 1)
                if L0:
                    mm = pe.matmul(ps_w[u % 2].rearrange("p j n -> p (j n)"), hidB[:, u % 2, :], mlp_out[:, :],
                                   start=True, stop=True)
                else:
                    for j in range(PAIR):
                        mm = pe.matmul(ps_w[u % 2][:, j, :], hidA[0:NH1, u % 2, j * P:(j + 1) * P], mlp_out[:, :],
                                       start=True, stop=True)
                mm.then_inc(w_ready, 1)

            def turn_messages(r, u):
                s = RING * r + u
                pe.wait_ge(mid_ready, s + 1)
                if not_first(r, u, 1):
                    pe.wait_ge(midT_ready, 2 * s)
                for j in range(PAIR):
                    for k in range(4):
                        mm = pe.transpose(ps_mid[j][0:widths[k], k, :],
                                          mid[:, u % 2, j, starts[k]:starts[k] + widths[k]], ident[:, :])
                    mm.then_inc(midT_psum, 1)

            def project(r, u):
                s = RING * r + u
                if not_first(r, u, 1):
                    pe.wait_ge(msg_ready, s)
                for j in range(PAIR):
                    pe.wait_ge(midT_ready, 2 * s + j + 1)
                    pe.matmul(ps_msg[:, j, 0:MUL_S], midT[0:96, j, 0, :], out_s[:, :], start=True, stop=True)
                    for c in range(3):
                        mm = pe.matmul(ps_msg[:, j, MUL_S + c * MUL_V:MUL_S + (c + 1) * MUL_V],
                                       midT[0:widths[1], j, 1 + c, :], out_v[:, :], start=True, stop=True)
                mm.then_inc(msg_psum, 1)

            def sum_same(r, u):
                s = RING * r + u
                if not_first(r, u, 1):
                    pe.wait_ge(sum_ready, s)
                pe.wait_ge(msg_ready, s + 1)
                for j in range(PAIR):
                    mm = pe.matmul(ps_sum[:, j, :], same[:, u, j, :], msg[:, j, :], start=True, stop=True)
                mm.then_inc(sum_psum, 1)

            def turn(r, u):
                if exists(*ahead(r, u, 3)):
                    turn_edges(*ahead(r, u, 3))
                if exists(*ahead(r, u, 2)):
                    hidden_a(*ahead(r, u, 2))
                if exists(r, u):
                    turn_messages(r, u)
                if L0 and exists(*ahead(r, u, 2)):
                    hidden_b(*ahead(r, u, 2))
                if exists(r, u):
                    project(r, u)
                if exists(*ahead(r, u, 2)):
                    edge_weights(*ahead(r, u, 2))
                if exists(r, u):
                    sum_same(r, u)
            run(pe, turn)

        @block.scalar
        def _(act):
            def targets(r, u):
                s = RING * r + u
                act.wait_ge(edges_loaded[u], 32 * r + 32)
                if not_first(r, u, RING):
                    act.wait_ge(dest_ready, s - RING + 1)
                act.activation(target[:, u, :], key[:, u, :, scatter_col], ACT.Copy).then_inc(target_ready, 1)

            def take_turned(r, u):
                s = RING * r + u
                act.wait_ge(turned, s + 1)
                if not_first(r, u, 2):
                    act.wait_ge(hA_ready, s - 1)
                act.activation(recT[:, u % 2, :], ps_turn[0:PAIR * REC, 0:P], ACT.Copy).then_inc(recT_ready, 1)

            def activate_a(r, u):
                s = RING * r + u
                act.wait_ge(hA_ready, s + 1)
                if not_first(r, u, 2):
                    act.wait_ge(hB_ready if L0 else w_ready, s - 1)
                if L0:
                    act.activation(hidA[:, u % 2, 0:P], ps_hA[:, 0:P], ACT.Silu, scale=NB0 ** -0.5).then_inc(actA_ready, 1)
                else:
                    act.activation(hidA[0:NH1, u % 2, :], ps_hA[0:NH1, :], ACT.Relu,
                                   scale=NB1 ** -0.5).then_inc(actA_ready, 1)

            def activate_b(r, u):
                s = RING * r + u
                act.wait_ge(hB_ready, s + 1)
                if not_first(r, u, 2):
                    act.wait_ge(w_ready, s - 1)
                act.activation(hidB[:, u % 2, :], ps_hB, ACT.Silu, scale=NH0 ** -0.5).then_inc(actB_ready, 1)

            def take_mid(r, u, j):
                s = RING * r + u
                act.wait_ge(midT_psum, 2 * s + j + 1)
                if not_first(r, u, 1):
                    act.wait_ge(msg_psum, s)
                if L0:
                    act.activation(midT[0:96, j, 0, :], ps_mid[j][0:96, 0, :], ACT.Copy)
                    act.activation(midT[:, j, 1:4, :], ps_mid[j][:, 1:4, :], ACT.Copy).then_inc(midT_ready, 1)
                else:
                    act.activation(midT[0:96, j, :, :], ps_mid[j][0:96, :, :], ACT.Copy).then_inc(midT_ready, 1)

            def take_msg(r, u):
                s = RING * r + u
                act.wait_ge(msg_psum, s + 1)
                if not_first(r, u, 1):
                    act.wait_ge(sum_psum, s)
                act.activation(msg[:, :, :], ps_msg, ACT.Copy).then_inc(msg_ready, 1)

            def take_sum(r, u):
                s = RING * r + u
                for j in range(PAIR):
                    c = PAIR * (u % 2) + j
                    if not_first(r, u, 2):
                        act.wait_ge(scattered[c], 32 * r + 16 * (u // 2))
                act.wait_ge(sum_psum, s + 1)
                act.activation(msg_sum[:, u % 2, :, :], ps_sum, ACT.Copy).then_inc(sum_ready, 1)

            def turn(r, u):
                if exists(*ahead(r, u, 2)):
                    activate_a(*ahead(r, u, 2))
                if exists(r, u):
                    take_mid(r, u, 0)
                if exists(*ahead(r, u, 3)):
                    take_turned(*ahead(r, u, 3))
                if exists(r, u):
                    take_mid(r, u, 1)
                if L0 and exists(*ahead(r, u, 2)):
                    activate_b(*ahead(r, u, 2))
                if exists(r, u):
                    take_msg(r, u)
                if exists(*ahead(r, u, 4)):
                    targets(*ahead(r, u, 4))
                if exists(r, u):
                    take_sum(r, u)
            run(act, turn)

        @block.vector
        def _(dve):
            def same_targets(r, u):
                s = RING * r + u
                dve.wait_ge(recT_ready, s + 1)
                if not_first(r, u, RING):
                    dve.wait_ge(sum_psum, s - RING + 1)
                dve.tensor_tensor(same[:, u, :, :], ps_turn[:, P:3 * P].rearrange("p (j e) -> p j e", j=PAIR),
                                  target[:, u, :].unsqueeze(2).broadcast_to([P, PAIR, P]),
                                  ALU.is_equal).then_inc(same_ready, 1)
                dve.wait_ge(same_ready, s + 1)
                for j in range(PAIR):
                    dve.scalar_tensor_tensor(junk[:, j, :], same[:, u, j, :], 1.0, before_mask[:, :], ALU.mult, ALU.mult,
                                             accum_out=before[:, u, j:j + 1]).then_inc(before_ready, 1)

            def destinations(r, u):
                s = RING * r + u
                for j in range(PAIR):
                    if not_first(r, u, RING):
                        dve.wait_ge(scattered[PAIR * (u % 2) + j], 32 * r + 16 * (u // 2) - 16)
                dve.wait_ge(before_ready, 2 * s + 2)
                dve.tensor_scalar(dump[:, u, :], before[:, u, :], 1.0, dump_row[:, 0:1], ALU.min,
                                  ALU.mult).then_inc(dump_ready, 1)
                dve.wait_ge(dump_ready, s + 1)
                dve.tensor_tensor(dest[:, u, :], dump[:, u, :], target[:, u, :], ALU.max).then_inc(dest_ready, 1)

            def products_0(r, u):
                s = RING * r + u
                b = u % 2
                done = 13 * s
                slots = outer[:, :, 0:480].rearrange("p j (a b n) -> p j a b n", a=3, b=5)
                flat = outer[:, :, 0:480].rearrange("p j (q n) -> p j q n", n=MUL_V)
                trace = outer[:, :, :].rearrange("p j (a m) -> p j a m", a=3)[:, :, :, 0:MUL_V]
                scal, vec = gath[:, u, :, 0:MUL_S], gath[:, u, :, MUL_S:D].rearrange("p j (a n) -> p j a n", a=3)
                sh = rec[:, u, :, SH:SH + 4]
                dve.wait_ge(edges_loaded[u], 32 * r + 32)
                dve.wait_ge(gathered[u], 32 * r + 32)
                if not_first(r, u, 1):
                    dve.wait_ge(mid_ready, s)
                for j in range(PAIR):
                    dve.tensor_tensor(slots[:, j, :, 0:4, :],
                                      vec[:, j, :, :].unsqueeze(2).broadcast_to([P, 3, 4, MUL_V]),
                                      sh[:, j, :].unsqueeze(1).unsqueeze(3).broadcast_to([P, 3, 4, MUL_V]),
                                      ALU.mult).then_inc(part, 1)
                dve.wait_ge(part, done + 2)
                for c in range(3):
                    a1, a2 = (c + 1) % 3, (c + 2) % 3
                    dve.tensor_tensor(flat[:, :, 5 * c + 4, :], flat[:, :, 5 * a1 + a2, :], flat[:, :, 5 * a2 + a1, :],
                                      ALU.subtract).then_inc(part, 1)
                dve.wait_ge(part, done + 5)
                dve.tensor_reduce(flat[:, :, 1, :], trace.rearrange("p j a n -> p j n a"), AX.X,
                                  ALU.add).then_inc(part, 1)
                if not_first(r, u, 2):
                    dve.wait_ge(midT_psum, 2 * s - 2)
                dve.wait_ge(w_ready, s + 1)
                wt = ps_w[b]
                dve.tensor_tensor(sw[:, :, :], wt[:, :, 64:128], scal, ALU.mult).then_inc(part, 1)
                for j in range(PAIR):
                    dve.scalar_tensor_tensor(scalars(b)[:, j, 0:MUL_S], wt[:, j, 0:64], sh[:, j, 3:4], scal[:, j, :],
                                             ALU.mult, ALU.mult).then_inc(part, 1)
                for j in range(PAIR):
                    dve.tensor_tensor(vectors(b)[:, j, :, 64:128], slots[:, j, :, 3:5, :].rearrange("p a b n -> p a (b n)"),
                                      wt[:, j, 128:192].unsqueeze(1).broadcast_to([P, 3, 64]),
                                      ALU.mult).then_inc(part, 1)
                dve.wait_ge(part, done + 11)
                dve.tensor_tensor(scalars(b)[:, :, MUL_S:96], wt[:, :, 192:224], flat[:, :, 1, :],
                                  ALU.mult).then_inc(part, 1)
                dve.tensor_tensor(vectors(b)[:, :, :, 0:64], sw[:, :, :].unsqueeze(2).broadcast_to([P, PAIR, 3, 64]),
                                  sh[:, :, 0:3].unsqueeze(3).broadcast_to([P, PAIR, 3, 64]),
                                  ALU.mult).then_inc(part, 1)
                dve.wait_ge(part, done + 13)
                dve.sem_inc(mid_ready, 1)

            def products_1(r, u):
                s = RING * r + u
                b = u % 2
                done = 10 * s
                ve = outer[:, :, 0:D_VEC].rearrange("p j (a n) -> p j a n", a=3)
                dot = outer[:, :, D_VEC:D_VEC + MUL_V]
                scal, vec = gath[:, u, :, 0:MUL_S], gath[:, u, :, MUL_S:D].rearrange("p j (a n) -> p j a n", a=3)
                sh = rec[:, u, :, SH:SH + 4]
                dve.wait_ge(edges_loaded[u], 32 * r + 32)
                dve.wait_ge(gathered[u], 32 * r + 32)
                if not_first(r, u, 1):
                    dve.wait_ge(mid_ready, s)
                dve.tensor_tensor(ve, vec, sh[:, :, 0:3].unsqueeze(3).broadcast_to([P, PAIR, 3, MUL_V]),
                                  ALU.mult).then_inc(part, 1)
                dve.wait_ge(part, done + 1)
                dve.tensor_reduce(dot, ve.rearrange("p j a n -> p j n a"), AX.X, ALU.add).then_inc(part, 1)
                if not_first(r, u, 2):
                    dve.wait_ge(midT_psum, 2 * s - 2)
                dve.wait_ge(w_ready, s + 1)
                wt = ps_w[b]
                dve.tensor_tensor(sw[:, :, :], wt[:, :, 64:128], scal, ALU.mult).then_inc(part, 1)
                for j in range(PAIR):
                    dve.scalar_tensor_tensor(scalars(b)[:, j, 0:MUL_S], wt[:, j, 0:64], sh[:, j, 3:4], scal[:, j, :],
                                             ALU.mult, ALU.mult).then_inc(part, 1)
                for j in range(PAIR):
                    dve.scalar_tensor_tensor(vectors(b)[:, j, :, 64:96], vec[:, j, :, :], sh[:, j, 3:4],
                                             wt[:, j, 128:160].unsqueeze(1).broadcast_to([P, 3, MUL_V]),
                                             ALU.mult, ALU.mult).then_inc(part, 1)
                dve.wait_ge(part, done + 7)
                dve.tensor_tensor(scalars(b)[:, :, MUL_S:96], wt[:, :, 160:192], dot, ALU.mult).then_inc(part, 1)
                dve.tensor_tensor(vectors(b)[:, :, :, 0:64], sw[:, :, :].unsqueeze(2).broadcast_to([P, PAIR, 3, 64]),
                                  sh[:, :, 0:3].unsqueeze(3).broadcast_to([P, PAIR, 3, 64]),
                                  ALU.mult).then_inc(part, 2)
                dve.wait_ge(part, done + 10)
                dve.sem_inc(mid_ready, 1)

            products = products_0 if L0 else products_1

            def turn(r, u):
                if exists(*ahead(r, u, 3)):
                    same_targets(*ahead(r, u, 3))
                if exists(*ahead(r, u, 1)):
                    destinations(*ahead(r, u, 1))
                    products(*ahead(r, u, 1))
            run(dve, turn)


def finish_layer(nc, layer, sem, X, skip, sums, stat, gains, node_vec, acc, out):
    loaded, done, roots, stored = (sem(f"f{layer}_{k}") for k in ("loaded", "done", "roots", "stored"))
    total = sums[:, 0, :, :]
    spare = sums[:, 1, :, :]
    scal, vec = slice(0, MUL_S), slice(MUL_S, D)

    def over(n, k):
        return stat[:, n, :].unsqueeze(2).broadcast_to([P, TILES, k])

    with nc.Block() as block:
        @block.sync
        def _(sp):
            for c in range(COPIES):
                sp.dma_start(sums[:, c, :, :], acc[c][0:NODES_PAD, :].rearrange("(t p) d -> p t d", p=P)).then_inc(loaded, 16)
            sp.wait_ge(loaded, 16 * COPIES)

        n = [0]

        @block.vector
        def _(dve):
            def step(ins):
                ins.then_inc(done, 1)
                n[0] += 1
                dve.wait_ge(done, n[0])

            dve.wait_ge(loaded, 16 * COPIES)
            step(dve.tensor_tensor(sums[:, 0, :, :], sums[:, 0, :, :], sums[:, 1, :, :], ALU.add))
            step(dve.tensor_tensor(sums[:, 2, :, :], sums[:, 2, :, :], sums[:, 3, :, :], ALU.add))
            step(dve.tensor_tensor(total, total, sums[:, 2, :, :], ALU.add))
            step(dve.tensor_tensor(total, total, skip[:, :, :], ALU.add))
            if layer == 1:
                step(dve.tensor_tensor(total, total, node_vec[:, :].unsqueeze(2).broadcast_to([P, TILES, D]), ALU.mult))
            if layer == 0:
                step(dve.tensor_tensor(spare, total, total, ALU.mult))
                step(dve.tensor_reduce(stat[:, 0, :], spare[:, :, scal], AX.X, ALU.add))
                step(dve.tensor_reduce(stat[:, 1, :], spare[:, :, vec], AX.X, ALU.add))
                step(dve.tensor_scalar(stat[:, 0, :], stat[:, 0, :], 1.0 / MUL_S, EPS, ALU.mult, ALU.add))
                step(dve.tensor_scalar(stat[:, 1, :], stat[:, 1, :], 1.0 / MUL_V, EPS, ALU.mult, ALU.add))
                dve.wait_ge(roots, 1)
                step(dve.reciprocal(stat[:, 2:4, :], stat[:, 2:4, :]))
                step(dve.tensor_tensor(total[:, :, scal], total[:, :, scal], over(2, MUL_S), ALU.mult))
                step(dve.tensor_tensor(total[:, :, vec], total[:, :, vec], over(3, D_VEC), ALU.mult))
                step(dve.tensor_tensor(total[:, :, scal], total[:, :, scal],
                                       gains[:, 0:MUL_S].unsqueeze(1).broadcast_to([P, TILES, MUL_S]), ALU.mult))
                tv = total[:, :, vec].rearrange("p t (c n) -> p t c n", c=3)
                step(dve.tensor_tensor(tv, tv, gains[:, MUL_S:].unsqueeze(1).unsqueeze(1)
                                       .broadcast_to([P, TILES, 3, MUL_V]), ALU.mult))
            step(dve.tensor_tensor(X[:, :, scal], X[:, :, scal], total[:, :, scal], ALU.add))
            xv = X[:, :, vec].rearrange("p t (n c) -> p t n c", c=3)
            step(dve.tensor_tensor(xv, xv, total[:, :, vec].rearrange("p t (c n) -> p t n c", c=3), ALU.add))
            step(dve.tensor_reduce(stat[:, 0, :], X[:, :, :], AX.X, ALU.add))
            step(dve.tensor_scalar(stat[:, 0, :], stat[:, 0, :], 1.0 / D, None, ALU.mult))
            step(dve.tensor_tensor(X[:, :, :], X[:, :, :], over(0, D), ALU.subtract))
            step(dve.tensor_tensor(spare, X[:, :, :], X[:, :, :], ALU.mult))
            step(dve.tensor_reduce(stat[:, 1, :], spare, AX.X, ALU.add))
            step(dve.tensor_scalar(stat[:, 1, :], stat[:, 1, :], 1.0 / D, EPS, ALU.mult, ALU.add))
            dve.wait_ge(roots, 2 if layer == 0 else 1)
            step(dve.reciprocal(stat[:, 3, :], stat[:, 3, :]))
            step(dve.tensor_tensor(X[:, :, :], X[:, :, :], over(3, D), ALU.mult))

        first_root = 9
        last = n[0]

        @block.scalar
        def _(act):
            if layer == 0:
                act.wait_ge(done, first_root)
                act.activation(stat[:, 2:4, :], stat[:, 0:2, :], ACT.Sqrt).then_inc(roots, 1)
            act.wait_ge(done, last - 2)
            act.activation(stat[:, 3, :], stat[:, 1, :], ACT.Sqrt).then_inc(roots, 1)
            if layer == 1:
                act.wait_ge(done, last)
                full = N_NODES // P
                act.dma_start(out[0:full * P, :].rearrange("(t p) d -> p t d", p=P), X[:, 0:full, :]).then_inc(stored, 16)
                act.dma_start(out[full * P:N_NODES, :], X[0:N_NODES - full * P, full, :]).then_inc(stored, 16)
                act.wait_ge(stored, 32)


WEIGHTS = ["node_s0", "node_v0", "mlp_in0", "mlp_mid0", "mlp_out0", "out_s0", "out_v0",
           "node_s1", "node_v1", "mlp_in1", "mlp_out1", "out_s1", "out_v1"]

_F0 = NH0 ** -0.5 * AVG
_F1 = (2.0 / NH1) ** 0.5 * AVG * 0.5 * 96 ** -0.5
SCALES = [
    ("node_s0", 0, MUL_S, MUL_S ** -0.5), ("node_v0", 0, D_VEC, MUL_V ** -0.5),
    ("node_s1", 0, MUL_S, MUL_S ** -0.5), ("node_v1", 0, D_VEC, MUL_V ** -0.5),
    ("out_s0", 0, 64, _F0 * 96 ** -0.5), ("out_s0", 64, 96, _F0 * 96 ** -0.5 * 3 ** -0.5),
    ("out_v0", 0, 96, _F0 * 128 ** -0.5), ("out_v0", 96, 128, _F0 * 128 ** -0.5 * 2 ** -0.5),
    ("out_s1", 0, 64, _F1), ("out_s1", 64, 96, _F1 * 3 ** -0.5), ("out_v1", 0, 96, _F1),
]


def kernel(x, src, dst, edge_attr_10, edge_attr_4, edge_attr_8, node_vec1, **p):
    import concourse.bacc as bacc
    from concourse.bass_utils import run_bass_kernel_spmd

    f = np.float32
    x = np.asarray(x)
    a = {k: np.asarray(v) for k, v in p.items()}
    arrays = {}
    arrays["x"] = np.zeros((NODES_PAD, D), f)
    arrays["x"][:N_NODES] = x
    node_vec = np.zeros(NODES_PAD, f)
    node_vec[:N_NODES] = np.asarray(node_vec1)[:, 0]
    arrays["node_vec"] = node_vec.reshape(TILES, P).T
    arrays["gains"] = np.concatenate([a["L0_gnn_g0"], a["L0_gnn_g1"]])
    sh = np.asarray(edge_attr_4)
    arrays["rec"] = np.zeros((EDGES_PAD, REC), f)
    arrays["rec"][:N_EDGES] = np.concatenate([np.asarray(edge_attr_8), np.asarray(edge_attr_10), sh[:, 1:4], sh[:, 0:1]], 1)
    arrays["keys"] = np.zeros((EDGES_PAD, 2), np.int32)
    arrays["keys"][:N_EDGES, 0] = np.asarray(src)
    arrays["keys"][:N_EDGES, 1] = np.asarray(dst)

    def per_component(m):
        b = np.zeros((MUL_V, 3, 3, MUL_V), f)
        for c in range(3):
            b[:, c, c, :] = m
        return b.reshape(D_VEC, D_VEC)

    for n, (s_msg, s_self, v_msg, v_self) in enumerate((("L0_gnn_W1_0", "L0_gnn_Wsc0", "L0_gnn_W1_1", "L0_gnn_Wsc1"),
                                                        ("L1_gnn_W_l1_0", "L1_gnn_W_si0", "L1_gnn_W_l1_1", "L1_gnn_W_si1"))):
        arrays[f"node_s{n}"] = np.concatenate([a[s_msg], a[s_self]], 1)
        arrays[f"node_v{n}"] = np.concatenate([per_component(a[v_msg]), per_component(a[v_self])], 1)
    arrays["mlp_in0"] = np.zeros((PAIR * REC, PAIR * NH0), f)
    arrays["mlp_mid0"] = np.zeros((PAIR * NH0, PAIR * NH0), f)
    arrays["mlp_in1"] = np.zeros((PAIR * REC, PAIR * NH1), f)
    for j in range(PAIR):
        arrays["mlp_in0"][j * REC:j * REC + NB0, j * NH0:(j + 1) * NH0] = a["L0_gnn_Wfc1"]
        arrays["mlp_mid0"][j * NH0:(j + 1) * NH0, j * NH0:(j + 1) * NH0] = a["L0_gnn_Wfc2"]
        arrays["mlp_in1"][j * REC + NB0:j * REC + NB0 + NB1, j * NH1:(j + 1) * NH1] = a["L1_gnn_W_fc1"]
    w3 = a["L0_gnn_Wfc3"]
    w3 = np.concatenate([w3[:, 0:160], w3[:, 192:224], w3[:, 160:192]], 1)
    arrays["mlp_out0"] = np.concatenate([np.pad(w3, ((0, 0), (224 * j, 224 * (PAIR - 1 - j)))) for j in range(PAIR)], 0)
    arrays["mlp_out1"] = a["L1_gnn_W_fc2"]
    arrays["out_s0"] = a["L0_gnn_W2_0"]
    arrays["out_v0"] = a["L0_gnn_W2_1"]
    arrays["out_s1"] = np.concatenate([a["L1_gnn_W_l2_00"], a["L1_gnn_W_l2_10"]], 0)
    arrays["out_v1"] = np.concatenate([a["L1_gnn_W_l2_01"], a["L1_gnn_W_l2_11"]], 0)
    arrays = {k: np.ascontiguousarray(v) for k, v in arrays.items()}

    nc = bacc.Bacc("TRN2", target_bir_lowering=False, num_devices=1)
    t_in = {k: nc.dram_tensor("in_" + k, v.shape, mybir.dt.from_np(v.dtype), kind="ExternalInput").ap()
            for k, v in arrays.items()}
    out = nc.dram_tensor("out", (N_NODES, D), F32, kind="ExternalOutput").ap()
    build(nc, t_in, out)
    r = run_bass_kernel_spmd(nc, [{"in_" + k: v for k, v in arrays.items()}], core_ids=[0])
    return r.results[0]["out"]
```

```python
from contextlib import ExitStack

import numpy as np

import concourse.bass as bass
import concourse.mybir as mybir
from concourse.alu_op_type import AluOpType as ALU

F32 = mybir.dt.float32
I32 = mybir.dt.int32
ACT = mybir.ActivationFunctionType
AX = mybir.AxisListType

P = 128
N_NODES = 3125
N_EDGES = 103125
MUL_S, MUL_V = 64, 32
D_VEC = 3 * MUL_V
D = MUL_S + D_VEC
TILES = -(-N_NODES // P)
NODES_PAD = TILES * P
GROUP = 5
PAIR = 2
STEP = PAIR * P
RING = 6
ROUNDS = -(-N_EDGES // (STEP * RING))
STEPS = ROUNDS * RING
EDGES_PAD = STEPS * STEP
NB0, NB1 = 8, 10
REC = NB0 + NB1 + 4
SH = NB0 + NB1
NH0, NH1 = 64, 100
COPIES = 4
ACC_ROWS = NODES_PAD + P
EPS = 1e-5
BANK = 512
AVG = 0.25


def build(nc, t_in, out):
    ctx = ExitStack()
    with ctx:
        def sb(name, shape, dt=F32):
            return ctx.enter_context(nc.sbuf_tensor(name, shape, dt))

        def sem(name):
            return ctx.enter_context(nc.semaphore(name))

        psum = ctx.enter_context(nc.psum_tensor("psum", [P, 8, BANK], F32))
        X = sb("X", [P, TILES, D])
        skip = sb("skip", [P, TILES, D])
        sums = sb("sums", [P, COPIES, TILES, D])
        stage = sb("stage", [P, GROUP, D])
        xTs = sb("xTs", [MUL_S, GROUP, P])
        xTv = sb("xTv", [D_VEC, GROUP, P])
        table_rows = sb("table_rows", [P, GROUP, D])
        stat = sb("stat", [P, 6, TILES])
        ident = sb("ident", [P, P])
        before_mask = sb("before_mask", [P, P])
        dump_row = sb("dump_row", [P, 1])
        dump_row_i = sb("dump_row_i", [P, 1], I32)
        node_vec = sb("node_vec", [P, TILES])
        gains = sb("gains", [P, D - 2 * MUL_V])
        rec = sb("rec", [P, RING, PAIR, REC])
        key = sb("key", [P, RING, PAIR, 2], I32)
        target = sb("target", [P, RING, PAIR])
        gath = sb("gath", [P, RING, PAIR, D])
        recT = sb("recT", [PAIR * REC, 2, P])
        hidA = sb("hidA", [P, 2, PAIR * P])
        hidB = sb("hidB", [P, 2, P])
        outer = sb("outer", [P, PAIR, 3 * 192])
        sw = sb("sw", [P, PAIR, MUL_S])
        mid = sb("mid", [P, 2, PAIR, 480])
        midT = sb("midT", [P, 2, PAIR, 4, P])
        same = sb("same", [P, RING, PAIR, P])
        junk = sb("junk", [P, PAIR, P])
        before = sb("before", [P, RING, PAIR])
        dump = sb("dump", [P, RING, PAIR])
        dest = sb("dest", [P, RING, PAIR], I32)
        msg = sb("msg", [P, 2, PAIR, D])
        msg_sum = sb("msg_sum", [P, 2, PAIR, D])
        w = {k: sb("w_" + k, list(t_in[k].shape)) for k in WEIGHTS}

        table = [nc.dram_tensor(f"table{n}", [NODES_PAD, D], F32, kind="Internal").ap() for n in range(2)]
        acc = [[nc.dram_tensor(f"acc{n}_{c}", [ACC_ROWS, D], F32, kind="Internal").ap() for c in range(COPIES)]
               for n in range(2)]

        loaded, zeroed = sem("loaded"), sem("zeroed")
        const, scaled = sem("const"), sem("scaled")
        with nc.Block() as block:
            @block.sync
            def _(sp):
                sp.dma_start(X[:, :, :], t_in["x"].rearrange("(t p) d -> p t d", p=P)).then_inc(loaded, 16)
                sp.dma_start(node_vec[:, :], t_in["node_vec"]).then_inc(loaded, 16)
                sp.dma_start(gains[:, :], t_in["gains"].unsqueeze(0).broadcast_to([P, MUL_S + MUL_V])).then_inc(loaded, 16)
                for k in WEIGHTS:
                    sp.dma_start(w[k][:, :], t_in[k]).then_inc(loaded, 16)
                sp.wait_ge(loaded, 16 * (3 + len(WEIGHTS)))

            @block.gpsimd
            def _(pool):
                pool.memset(ident[:, :], 0.0).then_inc(const, 1)
                pool.memset(before_mask[:, :], 1.0).then_inc(const, 1)
                pool.iota(dump_row_i[:, :], pattern=[[0, 1]], base=NODES_PAD, channel_multiplier=1).then_inc(const, 1)
                pool.wait_ge(const, 3)
                pool.affine_select(out=ident[:, :], in_=ident[:, :], compare_op=ALU.not_equal, fill=1.0, base=0,
                                   pattern=[[-1, P]], channel_multiplier=1).then_inc(const, 1)
                pool.affine_select(out=before_mask[:, :], in_=before_mask[:, :], compare_op=ALU.is_gt, fill=0.0,
                                   base=0, pattern=[[-1, P]], channel_multiplier=1).then_inc(const, 1)

            @block.vector
            def _(dve):
                dve.wait_ge(const, 5)
                dve.tensor_copy(dump_row[:, :], dump_row_i[:, :]).then_inc(const, 1)
                dve.memset(sums[:, 0, :, :], 0.0).then_inc(scaled, 1)
                dve.memset(sums[:, 1, 0, :], 0.0).then_inc(scaled, 1)
                dve.wait_ge(loaded, 16 * (3 + len(WEIGHTS)))
                for k, lo, hi, f in SCALES:
                    dve.tensor_scalar(w[k][lo:hi, :], w[k][lo:hi, :], f, None, ALU.mult).then_inc(scaled, 1)

            @block.scalar
            def _(act):
                act.wait_ge(scaled, 2)
                for n in range(2):
                    for c in range(COPIES):
                        act.dma_start(acc[n][c].rearrange("(p r) d -> p (r d)", p=P),
                                      sums[:, 0:2, :, :].rearrange("p c t d -> p (c t d)")[:, 0:ACC_ROWS // P * D],
                                      ).then_inc(zeroed, 16)
                act.wait_ge(zeroed, 16 * 2 * COPIES)

        for layer in range(2):
            node_projection(nc, layer, sem, psum, X, skip, stage, xTs, xTv, table_rows, ident, node_vec, w,
                            table[layer])
            edge_layer(nc, layer, sem, psum, t_in, rec, key, target, gath, recT, hidA, hidB, outer, sw, mid, midT,
                       same, junk, before, dump, dest, msg, msg_sum, before_mask, dump_row, ident, w,
                       table[layer], acc[layer])
            finish_layer(nc, layer, sem, X, skip, sums, stat, gains, node_vec, acc[layer], out)


def node_projection(nc, layer, sem, psum, X, skip, stage, xTs, xTv, table_rows, ident, node_vec, w, table):
    flat = psum[:, :, :].rearrange("p b c -> p (b c)")
    staged, turned, taken = sem(f"n{layer}_staged"), sem(f"n{layer}_turned"), sem(f"n{layer}_taken")
    projected, evacuated, stored = sem(f"n{layer}_projected"), sem(f"n{layer}_evacuated"), sem(f"n{layer}_stored")
    OUT = 3
    results = psum[:, OUT:OUT + GROUP, :]
    table_v = table.rearrange("(t p) d -> p t d", p=P)
    groups = TILES // GROUP
    per_group = 3

    with nc.Block() as block:
        @block.vector
        def _(dve):
            with dve.Fori(0, groups) as g:
                dve.wait_ge(turned, g)
                dve.tensor_copy(stage[:, :, :], X[:, bass.ds(g * GROUP, GROUP), :]).then_inc(staged, 1)
                dve.wait_ge(turned, g + 1)
                dve.tensor_copy(xTv[:, :, :].rearrange("k t n -> k (t n)"),
                                flat[0:D_VEC, 2 * BANK:2 * BANK + GROUP * P]).then_inc(taken, 1)
                dve.wait_ge(projected, g + 1)
                if layer == 0:
                    dve.wait_ge(evacuated, g * per_group + 2)
                dve.tensor_copy(skip[:, bass.ds(g * GROUP, GROUP), :], results[:, :, D:2 * D]).then_inc(evacuated, 1)
                if layer == 1:
                    a = node_vec[:, bass.ds(g * GROUP, GROUP)].unsqueeze(2).broadcast_to([P, GROUP, D])
                    dve.wait_ge(stored, 16 * g)
                    dve.tensor_tensor(table_rows[:, :, :], results[:, :, 0:D], a, ALU.mult).then_inc(evacuated, 2)

        @block.tensor
        def _(pe):
            with pe.Fori(0, groups) as g:
                pe.wait_ge(staged, g + 1)
                pe.wait_ge(evacuated, g * per_group)
                for k in range(GROUP):
                    pe.transpose(flat[0:D_VEC, 2 * BANK + k * P:2 * BANK + (k + 1) * P], stage[:, k, MUL_S:D], ident[:, :])
                    mm = pe.transpose(flat[0:MUL_S, k * P:(k + 1) * P], stage[:, k, 0:MUL_S], ident[:, :])
                mm.then_inc(turned, 1)
                pe.wait_ge(taken, 2 * g + 2)
                for k in range(GROUP):
                    for half in range(2):
                        ws = w[f"node_s{layer}"][:, half * MUL_S:(half + 1) * MUL_S]
                        wv = w[f"node_v{layer}"][:, half * D_VEC:(half + 1) * D_VEC]
                        pe.matmul(psum[:, OUT + k, half * D:half * D + MUL_S], xTs[:, k, :], ws, start=True, stop=True)
                        mm = pe.matmul(psum[:, OUT + k, half * D + MUL_S:(half + 1) * D], xTv[:, k, :], wv,
                                       start=True, stop=True)
                mm.then_inc(projected, 1)

        @block.scalar
        def _(act):
            with act.Fori(0, groups) as g:
                act.wait_ge(turned, g + 1)
                act.activation(xTs[:, :, :].rearrange("k t n -> k (t n)"), flat[0:MUL_S, 0:GROUP * P],
                               ACT.Copy).then_inc(taken, 1)
                if layer == 0:
                    act.wait_ge(projected, g + 1)
                    act.wait_ge(stored, 16 * g)
                    act.activation(table_rows[:, :, :], results[:, :, 0:D], ACT.Copy).then_inc(evacuated, 2)

        @block.sync
        def _(sp):
            with sp.Fori(0, groups) as g:
                sp.wait_ge(evacuated, g * per_group + per_group)
                sp.dma_start(table_v[:, bass.ds(g * GROUP, GROUP), :], table_rows[:, :, :]).then_inc(stored, 16)
            sp.wait_ge(stored, 16 * groups)


def edge_layer(nc, layer, sem, psum, t_in, rec, key, target, gath, recT, hidA, hidB, outer, sw, mid, midT,
               same, junk, before, dump, dest, msg, msg_sum, before_mask, dump_row, ident, w, table, acc):
    L0 = layer == 0
    gather_col, scatter_col = (1, 0) if L0 else (0, 1)
    hidden = NH0 if L0 else NH1
    n_w = 224 if L0 else 192
    widths = [96, 128, 128, 128] if L0 else [96] * 4
    n_mid = sum(widths)
    PARTS = 13 if L0 else 9
    starts = [sum(widths[:k]) for k in range(4)]
    out_s, out_v = w[f"out_s{layer}"], w[f"out_v{layer}"]
    mlp_in, mlp_out = w[f"mlp_in{layer}"], w[f"mlp_out{layer}"]
    rows_v = t_in["rec"].rearrange("(s p j) f -> s p (j f)", p=P, j=PAIR)
    keys_v = t_in["keys"].rearrange("(s p j) f -> s p (j f)", p=P, j=PAIR)

    def name(what):
        return sem(f"e{layer}_{what}")

    edges_loaded = [name(f"edges_loaded{u}") for u in range(RING)]
    gathered = [name(f"gathered{u}") for u in range(RING)]
    scattered = [name(f"scattered{c}") for c in range(COPIES)]
    target_ready, turned, recT_ready = name("target_ready"), name("turned"), name("recT_ready")
    hA_ready, actA_ready, hB_ready, actB_ready = name("hA"), name("actA"), name("hB"), name("actB")
    w_ready, midT_psum, midT_ready = name("w"), name("midT_psum"), name("midT")
    msg_psum, msg_ready, sum_psum, sum_ready = name("msg_psum"), name("msg"), name("sum_psum"), name("sum")
    same_ready, before_ready, dump_ready, dest_ready = name("same"), name("before"), name("dump"), name("dest")
    part = name("part")
    pool_turns = name("pool_turns")

    ps_turn = psum[:, 0, :]
    ps_hA = psum[:, 1, 0:PAIR * P]
    ps_hB = psum[:, 1, PAIR * P:PAIR * P + P]
    ps_w = [psum[:, 2 + b, 0:PAIR * n_w].rearrange("p (j n) -> p j n", j=PAIR) for b in range(2)]
    ps_mid = [psum[:, 4 + j, :].rearrange("p (k e) -> p k e", k=4) for j in range(PAIR)]
    ps_msg = psum[:, 6, 0:PAIR * D].rearrange("p (j d) -> p j d", j=PAIR)
    ps_sum = psum[:, 7, 0:PAIR * D].rearrange("p (j d) -> p j d", j=PAIR)

    def ahead(r, u, k):
        return r + (u + k) // RING, (u + k) % RING

    def exists(r, u):
        return not isinstance(r, int) or 0 <= RING * r + u < STEPS

    def not_first(r, u, depth):
        return not isinstance(r, int) or RING * r + u >= depth

    def uses(r, u):
        return RING // 2 * r + u // 2

    def run(eng, turn):
        for r in (-1, 0):
            for u in range(RING):
                turn(r, u)
        with eng.Fori(1, ROUNDS - 1) as r:
            for u in range(RING):
                turn(r, u)
        for r in (ROUNDS - 1, ROUNDS):
            for u in range(RING):
                turn(r, u)

    def scalars(b):
        return mid[:, b, :, 0:96]

    def vectors(b):
        return mid[:, b, :, 96:n_mid].rearrange("p j (c n) -> p j c n", c=3)

    with nc.Block() as block:
        @block.sync
        def _(sp):
            def load(r, u):
                s = RING * r + u
                if not_first(r, u, RING):
                    sp.wait_ge(part, PARTS * (s - RING + 1))
                sp.dma_start(rec[:, u, :, :].rearrange("p j f -> p (j f)"),
                             rows_v[bass.ds(s, 1), :, :].rearrange("s p f -> (s p) f")).then_inc(edges_loaded[u], 16)
                sp.dma_start(key[:, u, :, :].rearrange("p j f -> p (j f)"),
                             keys_v[bass.ds(s, 1), :, :].rearrange("s p f -> (s p) f")).then_inc(edges_loaded[u], 16)
            for u in range(RING):
                load(0, u)
            with sp.Fori(1, ROUNDS) as r:
                for u in range(RING):
                    load(r, u)

        @block.gpsimd
        def _(pool):
            def gather(r, u):
                s = RING * r + u
                pool.wait_ge(edges_loaded[u], 32 * r + 32)
                if not_first(r, u, RING):
                    pool.wait_ge(part, PARTS * (s - RING + 1))
                pool.sem_inc(pool_turns, 1)
                for j in range(PAIR):
                    pool.indirect_dma_start(
                        gath[:, u, j, :], None, table,
                        bass.IndirectOffsetOnAxis(ap=key[:, u, j, gather_col:gather_col + 1], axis=0),
                    ).then_inc(gathered[u], 16)

            def scatter(r, u):
                s = RING * r + u
                pool.wait_ge(sum_ready, s + 1)
                pool.wait_ge(dest_ready, s + 1)
                for j in range(PAIR):
                    c = PAIR * (u % 2) + j
                    if not_first(r, u, 2):
                        pool.wait_ge(scattered[c], 16 * uses(r, u))
                pool.sem_inc(pool_turns, 1)
                for j in range(PAIR):
                    c = PAIR * (u % 2) + j
                    pool.indirect_dma_start(
                        acc[c], bass.IndirectOffsetOnAxis(ap=dest[:, u, j:j + 1], axis=0),
                        msg_sum[:, u % 2, j, :], None, compute_op=ALU.add,
                    ).then_inc(scattered[c], 16)

            def turn(r, u):
                if exists(*ahead(r, u, 3)):
                    gather(*ahead(r, u, 3))
                if exists(*ahead(r, u, -2)):
                    scatter(*ahead(r, u, -2))
            run(pool, turn)
            for c in range(COPIES):
                pool.wait_ge(scattered[c], 16 * STEPS // 2)

        @block.tensor
        def _(pe):
            def turn_edges(r, u):
                s = RING * r + u
                pe.wait_ge(edges_loaded[u], 32 * r + 32)
                if not_first(r, u, 1):
                    pe.wait_ge(same_ready, s)
                pe.wait_ge(target_ready, s + 1)
                for j in range(PAIR):
                    pe.transpose(ps_turn[:, P * (1 + j):P * (2 + j)], target[:, u, j:j + 1].broadcast_to([P, P]),
                                 ident[:, :])
                mm = pe.transpose(ps_turn[0:PAIR * REC, 0:P], rec[:, u, :, :].rearrange("p j f -> p (j f)"), ident[:, :])
                mm.then_inc(turned, 1)

            def hidden_a(r, u):
                s = RING * r + u
                if not_first(r, u, 1):
                    pe.wait_ge(actB_ready if L0 else actA_ready, s)
                pe.wait_ge(recT_ready, s + 1)
                if L0:
                    mm = pe.matmul(ps_hA[:, 0:P], mlp_in[:, :], recT[:, u % 2, :], start=True, stop=True)
                else:
                    for j in range(PAIR):
                        mm = pe.matmul(ps_hA[0:NH1, j * P:(j + 1) * P], mlp_in[:, j * NH1:(j + 1) * NH1],
                                       recT[:, u % 2, :], start=True, stop=True)
                mm.then_inc(hA_ready, 1)

            def hidden_b(r, u):
                s = RING * r + u
                pe.wait_ge(actA_ready, s + 1)
                pe.matmul(ps_hB, w["mlp_mid0"][:, :], hidA[:, u % 2, 0:P], start=True, stop=True).then_inc(hB_ready, 1)

            def edge_weights(r, u):
                s = RING * r + u
                if not_first(r, u, 2):
                    pe.wait_ge(part, PARTS * (s - 1))
                pe.wait_ge(actB_ready if L0 else actA_ready, s + 1)
                if L0:
                    mm = pe.matmul(ps_w[u % 2].rearrange("p j n -> p (j n)"), hidB[:, u % 2, :], mlp_out[:, :],
                                   start=True, stop=True)
                else:
                    for j in range(PAIR):
                        mm = pe.matmul(ps_w[u % 2][:, j, :], hidA[0:NH1, u % 2, j * P:(j + 1) * P], mlp_out[:, :],
                                       start=True, stop=True)
                mm.then_inc(w_ready, 1)

            def turn_messages(r, u):
                s = RING * r + u
                if not_first(r, u, 1):
                    pe.wait_ge(midT_ready, 2 * s)
                pe.wait_ge(part, PARTS * (s + 1))
                for j in range(PAIR):
                    for k in range(4):
                        mm = pe.transpose(ps_mid[j][0:widths[k], k, :],
                                          mid[:, u % 2, j, starts[k]:starts[k] + widths[k]], ident[:, :])
                    mm.then_inc(midT_psum, 1)

            def project(r, u):
                s = RING * r + u
                if not_first(r, u, 1):
                    pe.wait_ge(msg_ready, s)
                for j in range(PAIR):
                    pe.wait_ge(midT_ready, 2 * s + j + 1)
                    pe.matmul(ps_msg[:, j, 0:MUL_S], midT[0:96, u % 2, j, 0, :], out_s[:, :], start=True, stop=True)
                    for c in range(3):
                        mm = pe.matmul(ps_msg[:, j, MUL_S + c * MUL_V:MUL_S + (c + 1) * MUL_V],
                                       midT[0:widths[1], u % 2, j, 1 + c, :], out_v[:, :], start=True, stop=True)
                mm.then_inc(msg_psum, 1)

            def sum_same(r, u):
                s = RING * r + u
                if not_first(r, u, 1):
                    pe.wait_ge(sum_ready, s)
                pe.wait_ge(msg_ready, s + 1)
                for j in range(PAIR):
                    mm = pe.matmul(ps_sum[:, j, :], same[:, u, j, :], msg[:, u % 2, j, :], start=True, stop=True)
                mm.then_inc(sum_psum, 1)

            def turn(r, u):
                if exists(*ahead(r, u, 2)):
                    hidden_a(*ahead(r, u, 2))
                if exists(*ahead(r, u, -1)):
                    project(*ahead(r, u, -1))
                if L0 and exists(*ahead(r, u, 2)):
                    hidden_b(*ahead(r, u, 2))
                if exists(r, u):
                    turn_messages(r, u)
                if exists(*ahead(r, u, 2)):
                    edge_weights(*ahead(r, u, 2))
                if exists(*ahead(r, u, 3)):
                    turn_edges(*ahead(r, u, 3))
                if exists(*ahead(r, u, -2)):
                    sum_same(*ahead(r, u, -2))
            run(pe, turn)

        @block.scalar
        def _(act):
            def targets(r, u):
                s = RING * r + u
                act.wait_ge(edges_loaded[u], 32 * r + 32)
                if not_first(r, u, RING):
                    act.wait_ge(dest_ready, s - RING + 1)
                act.activation(target[:, u, :], key[:, u, :, scatter_col], ACT.Copy).then_inc(target_ready, 1)

            def take_turned(r, u):
                s = RING * r + u
                act.wait_ge(turned, s + 1)
                if not_first(r, u, 2):
                    act.wait_ge(hA_ready, s - 1)
                act.activation(recT[:, u % 2, :], ps_turn[0:PAIR * REC, 0:P], ACT.Copy).then_inc(recT_ready, 1)

            def activate_a(r, u):
                s = RING * r + u
                act.wait_ge(hA_ready, s + 1)
                if not_first(r, u, 2):
                    act.wait_ge(hB_ready if L0 else w_ready, s - 1)
                if L0:
                    act.activation(hidA[:, u % 2, 0:P], ps_hA[:, 0:P], ACT.Silu, scale=NB0 ** -0.5).then_inc(actA_ready, 1)
                else:
                    act.activation(hidA[0:NH1, u % 2, :], ps_hA[0:NH1, :], ACT.Relu,
                                   scale=NB1 ** -0.5).then_inc(actA_ready, 1)

            def activate_b(r, u):
                s = RING * r + u
                act.wait_ge(hB_ready, s + 1)
                if not_first(r, u, 2):
                    act.wait_ge(w_ready, s - 1)
                act.activation(hidB[:, u % 2, :], ps_hB, ACT.Silu, scale=NH0 ** -0.5).then_inc(actB_ready, 1)

            def take_mid(r, u, j):
                s = RING * r + u
                act.wait_ge(midT_psum, 2 * s + j + 1)
                if not_first(r, u, 2):
                    act.wait_ge(msg_psum, s - 1)
                if L0:
                    act.activation(midT[0:96, u % 2, j, 0, :], ps_mid[j][0:96, 0, :], ACT.Copy)
                    act.activation(midT[:, u % 2, j, 1:4, :], ps_mid[j][:, 1:4, :], ACT.Copy).then_inc(midT_ready, 1)
                else:
                    act.activation(midT[0:96, u % 2, j, :, :], ps_mid[j][0:96, :, :], ACT.Copy).then_inc(midT_ready, 1)

            def take_msg(r, u):
                s = RING * r + u
                act.wait_ge(msg_psum, s + 1)
                if not_first(r, u, 2):
                    act.wait_ge(sum_psum, s - 1)
                act.activation(msg[:, u % 2, :, :], ps_msg, ACT.Copy).then_inc(msg_ready, 1)

            def take_sum(r, u):
                s = RING * r + u
                for j in range(PAIR):
                    c = PAIR * (u % 2) + j
                    if not_first(r, u, 2):
                        act.wait_ge(scattered[c], 16 * uses(r, u))
                act.wait_ge(sum_psum, s + 1)
                act.activation(msg_sum[:, u % 2, :, :], ps_sum, ACT.Copy).then_inc(sum_ready, 1)

            def turn(r, u):
                if exists(*ahead(r, u, 4)):
                    targets(*ahead(r, u, 4))
                if exists(*ahead(r, u, 2)):
                    activate_a(*ahead(r, u, 2))
                if exists(*ahead(r, u, -1)):
                    take_msg(*ahead(r, u, -1))
                if L0 and exists(*ahead(r, u, 2)):
                    activate_b(*ahead(r, u, 2))
                for j in range(PAIR):
                    if exists(r, u):
                        take_mid(r, u, j)
                if exists(*ahead(r, u, 3)):
                    take_turned(*ahead(r, u, 3))
                if exists(*ahead(r, u, -2)):
                    take_sum(*ahead(r, u, -2))
            run(act, turn)

        @block.vector
        def _(dve):
            def same_targets(r, u):
                s = RING * r + u
                dve.wait_ge(recT_ready, s + 1)
                if not_first(r, u, RING):
                    dve.wait_ge(sum_psum, s - RING + 1)
                dve.tensor_tensor(same[:, u, :, :], ps_turn[:, P:3 * P].rearrange("p (j e) -> p j e", j=PAIR),
                                  target[:, u, :].unsqueeze(2).broadcast_to([P, PAIR, P]),
                                  ALU.is_equal).then_inc(same_ready, 1)

            def count_before(r, u):
                s = RING * r + u
                dve.wait_ge(same_ready, s + 1)
                if not_first(r, u, 1):
                    dve.wait_ge(before_ready, 2 * s)
                for j in range(PAIR):
                    dve.scalar_tensor_tensor(junk[:, j, :], same[:, u, j, :], 1.0, before_mask[:, :], ALU.mult, ALU.mult,
                                             accum_out=before[:, u, j:j + 1]).then_inc(before_ready, 1)

            def dump_rows(r, u):
                s = RING * r + u
                dve.wait_ge(before_ready, 2 * s + 2)
                dve.tensor_scalar(dump[:, u, :], before[:, u, :], 1.0, dump_row[:, 0:1], ALU.min,
                                  ALU.mult).then_inc(dump_ready, 1)

            def destinations(r, u):
                s = RING * r + u
                for j in range(PAIR):
                    if not_first(r, u, RING):
                        dve.wait_ge(scattered[PAIR * (u % 2) + j], 16 * (uses(r, u) - RING // 2 + 1))
                dve.wait_ge(dump_ready, s + 1)
                dve.tensor_tensor(dest[:, u, :], dump[:, u, :], target[:, u, :], ALU.max).then_inc(dest_ready, 1)

            def views(r, u):
                b = u % 2
                scal, vec = gath[:, u, :, 0:MUL_S], gath[:, u, :, MUL_S:D].rearrange("p j (a n) -> p j a n", a=3)
                return scal, vec, rec[:, u, :, SH:SH + 4], ps_w[b], scalars(b), vectors(b)

            def weighted_scalars(r, u):
                s = RING * r + u
                scal, _, sh, wt, mid_s, _ = views(r, u)
                if not_first(r, u, 2):
                    dve.wait_ge(midT_psum, 2 * s - 2)
                dve.wait_ge(w_ready, s + 1)
                dve.tensor_tensor(sw[:, :, :], wt[:, :, 64:128], scal, ALU.mult).then_inc(part, 1)
                for j in range(PAIR):
                    dve.scalar_tensor_tensor(mid_s[:, j, 0:MUL_S], wt[:, j, 0:64], sh[:, j, 3:4], scal[:, j, :],
                                             ALU.mult, ALU.mult).then_inc(part, 1)

            def spread_scalars(r, u):
                _, _, sh, _, _, mid_v = views(r, u)
                dve.tensor_tensor(mid_v[:, :, :, 0:64], sw[:, :, :].unsqueeze(2).broadcast_to([P, PAIR, 3, 64]),
                                  sh[:, :, 0:3].unsqueeze(3).broadcast_to([P, PAIR, 3, 64]),
                                  ALU.mult).then_inc(part, 1)

            def turn_0(a, b):
                slots = outer[:, :, 0:480].rearrange("p j (a b n) -> p j a b n", a=3, b=5)
                flat = outer[:, :, 0:480].rearrange("p j (q n) -> p j q n", n=MUL_V)
                trace = outer[:, :, :].rearrange("p j (a m) -> p j a m", a=3)[:, :, :, 0:MUL_V]
                if b:
                    same_targets(*b)
                if a:
                    r, u = a
                    s = RING * r + u
                    done = PARTS * s
                    _, vec, sh, wt, mid_s, mid_v = views(r, u)
                    dve.wait_ge(edges_loaded[u], 32 * r + 32)
                    dve.wait_ge(gathered[u], 32 * r + 32)
                    if not_first(r, u, 1):
                        dve.wait_ge(part, done)
                    for j in range(PAIR):
                        dve.tensor_tensor(slots[:, j, :, 0:4, :],
                                          vec[:, j, :, :].unsqueeze(2).broadcast_to([P, 3, 4, MUL_V]),
                                          sh[:, j, :].unsqueeze(1).unsqueeze(3).broadcast_to([P, 3, 4, MUL_V]),
                                          ALU.mult).then_inc(part, 1)
                if b:
                    count_before(*b)
                if a:
                    dve.wait_ge(part, done + 2)
                    for c in range(3):
                        a1, a2 = (c + 1) % 3, (c + 2) % 3
                        dve.tensor_tensor(flat[:, :, 5 * c + 4, :], flat[:, :, 5 * a1 + a2, :],
                                          flat[:, :, 5 * a2 + a1, :], ALU.subtract).then_inc(part, 1)
                    weighted_scalars(r, u)
                    dve.wait_ge(part, done + 5)
                    dve.tensor_reduce(flat[:, :, 1, :], trace.rearrange("p j a n -> p j n a"), AX.X,
                                      ALU.add).then_inc(part, 1)
                    for j in range(PAIR):
                        dve.tensor_tensor(mid_v[:, j, :, 64:128], slots[:, j, :, 3:5, :].rearrange("p a b n -> p a (b n)"),
                                          wt[:, j, 128:192].unsqueeze(1).broadcast_to([P, 3, 64]),
                                          ALU.mult).then_inc(part, 1)
                if b:
                    dump_rows(*b)
                if a:
                    dve.wait_ge(part, done + 9)
                    dve.tensor_tensor(mid_s[:, :, MUL_S:96], wt[:, :, 192:224], flat[:, :, 1, :],
                                      ALU.mult).then_inc(part, 1)
                    spread_scalars(r, u)
                    destinations(r, u)

            def turn_1(a, b):
                ve = outer[:, :, 0:D_VEC].rearrange("p j (a n) -> p j a n", a=3)
                dot = outer[:, :, D_VEC:D_VEC + MUL_V]
                if b:
                    same_targets(*b)
                if a:
                    r, u = a
                    s = RING * r + u
                    done = PARTS * s
                    _, vec, sh, wt, mid_s, mid_v = views(r, u)
                    dve.wait_ge(edges_loaded[u], 32 * r + 32)
                    dve.wait_ge(gathered[u], 32 * r + 32)
                    if not_first(r, u, 1):
                        dve.wait_ge(part, done)
                    dve.tensor_tensor(ve, vec, sh[:, :, 0:3].unsqueeze(3).broadcast_to([P, PAIR, 3, MUL_V]),
                                      ALU.mult).then_inc(part, 1)
                if b:
                    count_before(*b)
                if a:
                    weighted_scalars(r, u)
                    dve.wait_ge(part, done + 1)
                    dve.tensor_reduce(dot, ve.rearrange("p j a n -> p j n a"), AX.X, ALU.add).then_inc(part, 1)
                    for j in range(PAIR):
                        dve.scalar_tensor_tensor(mid_v[:, j, :, 64:96], vec[:, j, :, :], sh[:, j, 3:4],
                                                 wt[:, j, 128:160].unsqueeze(1).broadcast_to([P, 3, MUL_V]),
                                                 ALU.mult, ALU.mult).then_inc(part, 1)
                if b:
                    dump_rows(*b)
                if a:
                    dve.wait_ge(part, done + 5)
                    dve.tensor_tensor(mid_s[:, :, MUL_S:96], wt[:, :, 160:192], dot, ALU.mult).then_inc(part, 1)
                    spread_scalars(r, u)
                    destinations(r, u)

            def turn(r, u):
                a, b = ahead(r, u, 1), ahead(r, u, 2)
                (turn_0 if L0 else turn_1)(a if exists(*a) else None, b if exists(*b) else None)
            run(dve, turn)


def finish_layer(nc, layer, sem, X, skip, sums, stat, gains, node_vec, acc, out):
    loaded, done, roots, stored = (sem(f"f{layer}_{k}") for k in ("loaded", "done", "roots", "stored"))
    total = sums[:, 0, :, :]
    spare = sums[:, 1, :, :]
    scal, vec = slice(0, MUL_S), slice(MUL_S, D)

    def over(n, k):
        return stat[:, n, :].unsqueeze(2).broadcast_to([P, TILES, k])

    with nc.Block() as block:
        @block.sync
        def _(sp):
            for c in range(COPIES):
                sp.dma_start(sums[:, c, :, :], acc[c][0:NODES_PAD, :].rearrange("(t p) d -> p t d", p=P)).then_inc(loaded, 16)
            sp.wait_ge(loaded, 16 * COPIES)

        n = [0]

        @block.vector
        def _(dve):
            def step(ins):
                ins.then_inc(done, 1)
                n[0] += 1
                dve.wait_ge(done, n[0])

            dve.wait_ge(loaded, 16 * COPIES)
            step(dve.tensor_tensor(sums[:, 0, :, :], sums[:, 0, :, :], sums[:, 1, :, :], ALU.add))
            step(dve.tensor_tensor(sums[:, 2, :, :], sums[:, 2, :, :], sums[:, 3, :, :], ALU.add))
            step(dve.tensor_tensor(total, total, sums[:, 2, :, :], ALU.add))
            step(dve.tensor_tensor(total, total, skip[:, :, :], ALU.add))
            if layer == 1:
                step(dve.tensor_tensor(total, total, node_vec[:, :].unsqueeze(2).broadcast_to([P, TILES, D]), ALU.mult))
            if layer == 0:
                step(dve.tensor_tensor(spare, total, total, ALU.mult))
                step(dve.tensor_reduce(stat[:, 0, :], spare[:, :, scal], AX.X, ALU.add))
                step(dve.tensor_reduce(stat[:, 1, :], spare[:, :, vec], AX.X, ALU.add))
                step(dve.tensor_scalar(stat[:, 0, :], stat[:, 0, :], 1.0 / MUL_S, EPS, ALU.mult, ALU.add))
                step(dve.tensor_scalar(stat[:, 1, :], stat[:, 1, :], 1.0 / MUL_V, EPS, ALU.mult, ALU.add))
                dve.wait_ge(roots, 1)
                step(dve.reciprocal(stat[:, 2:4, :], stat[:, 2:4, :]))
                step(dve.tensor_tensor(total[:, :, scal], total[:, :, scal], over(2, MUL_S), ALU.mult))
                step(dve.tensor_tensor(total[:, :, vec], total[:, :, vec], over(3, D_VEC), ALU.mult))
                step(dve.tensor_tensor(total[:, :, scal], total[:, :, scal],
                                       gains[:, 0:MUL_S].unsqueeze(1).broadcast_to([P, TILES, MUL_S]), ALU.mult))
                tv = total[:, :, vec].rearrange("p t (c n) -> p t c n", c=3)
                step(dve.tensor_tensor(tv, tv, gains[:, MUL_S:].unsqueeze(1).unsqueeze(1)
                                       .broadcast_to([P, TILES, 3, MUL_V]), ALU.mult))
            step(dve.tensor_tensor(X[:, :, scal], X[:, :, scal], total[:, :, scal], ALU.add))
            xv = X[:, :, vec].rearrange("p t (n c) -> p t n c", c=3)
            step(dve.tensor_tensor(xv, xv, total[:, :, vec].rearrange("p t (c n) -> p t n c", c=3), ALU.add))
            step(dve.tensor_reduce(stat[:, 0, :], X[:, :, :], AX.X, ALU.add))
            step(dve.tensor_scalar(stat[:, 0, :], stat[:, 0, :], 1.0 / D, None, ALU.mult))
            step(dve.tensor_tensor(X[:, :, :], X[:, :, :], over(0, D), ALU.subtract))
            step(dve.tensor_tensor(spare, X[:, :, :], X[:, :, :], ALU.mult))
            step(dve.tensor_reduce(stat[:, 1, :], spare, AX.X, ALU.add))
            step(dve.tensor_scalar(stat[:, 1, :], stat[:, 1, :], 1.0 / D, EPS, ALU.mult, ALU.add))
            dve.wait_ge(roots, 2 if layer == 0 else 1)
            step(dve.reciprocal(stat[:, 3, :], stat[:, 3, :]))
            step(dve.tensor_tensor(X[:, :, :], X[:, :, :], over(3, D), ALU.mult))

        first_root = 9
        last = n[0]

        @block.scalar
        def _(act):
            if layer == 0:
                act.wait_ge(done, first_root)
                act.activation(stat[:, 2:4, :], stat[:, 0:2, :], ACT.Sqrt).then_inc(roots, 1)
            act.wait_ge(done, last - 2)
            act.activation(stat[:, 3, :], stat[:, 1, :], ACT.Sqrt).then_inc(roots, 1)
            if layer == 1:
                act.wait_ge(done, last)
                full = N_NODES // P
                act.dma_start(out[0:full * P, :].rearrange("(t p) d -> p t d", p=P), X[:, 0:full, :]).then_inc(stored, 16)
                act.dma_start(out[full * P:N_NODES, :], X[0:N_NODES - full * P, full, :]).then_inc(stored, 16)
                act.wait_ge(stored, 32)


WEIGHTS = ["node_s0", "node_v0", "mlp_in0", "mlp_mid0", "mlp_out0", "out_s0", "out_v0",
           "node_s1", "node_v1", "mlp_in1", "mlp_out1", "out_s1", "out_v1"]

_F0 = NH0 ** -0.5 * AVG
_F1 = (2.0 / NH1) ** 0.5 * AVG * 0.5 * 96 ** -0.5
SCALES = [
    ("node_s0", 0, MUL_S, MUL_S ** -0.5), ("node_v0", 0, D_VEC, MUL_V ** -0.5),
    ("node_s1", 0, MUL_S, MUL_S ** -0.5), ("node_v1", 0, D_VEC, MUL_V ** -0.5),
    ("out_s0", 0, 64, _F0 * 96 ** -0.5), ("out_s0", 64, 96, _F0 * 96 ** -0.5 * 3 ** -0.5),
    ("out_v0", 0, 96, _F0 * 128 ** -0.5), ("out_v0", 96, 128, _F0 * 128 ** -0.5 * 2 ** -0.5),
    ("out_s1", 0, 64, _F1), ("out_s1", 64, 96, _F1 * 3 ** -0.5), ("out_v1", 0, 96, _F1),
]


def kernel(x, src, dst, edge_attr_10, edge_attr_4, edge_attr_8, node_vec1, **p):
    import concourse.bacc as bacc
    from concourse.bass_utils import run_bass_kernel_spmd

    f = np.float32
    x = np.asarray(x)
    a = {k: np.asarray(v) for k, v in p.items()}
    arrays = {}
    arrays["x"] = np.zeros((NODES_PAD, D), f)
    arrays["x"][:N_NODES] = x
    node_vec = np.zeros(NODES_PAD, f)
    node_vec[:N_NODES] = np.asarray(node_vec1)[:, 0]
    arrays["node_vec"] = node_vec.reshape(TILES, P).T
    arrays["gains"] = np.concatenate([a["L0_gnn_g0"], a["L0_gnn_g1"]])
    sh = np.asarray(edge_attr_4)
    arrays["rec"] = np.zeros((EDGES_PAD, REC), f)
    arrays["rec"][:N_EDGES] = np.concatenate([np.asarray(edge_attr_8), np.asarray(edge_attr_10), sh[:, 1:4], sh[:, 0:1]], 1)
    arrays["keys"] = np.zeros((EDGES_PAD, 2), np.int32)
    arrays["keys"][:N_EDGES, 0] = np.asarray(src)
    arrays["keys"][:N_EDGES, 1] = np.asarray(dst)

    def per_component(m):
        b = np.zeros((MUL_V, 3, 3, MUL_V), f)
        for c in range(3):
            b[:, c, c, :] = m
        return b.reshape(D_VEC, D_VEC)

    for n, (s_msg, s_self, v_msg, v_self) in enumerate((("L0_gnn_W1_0", "L0_gnn_Wsc0", "L0_gnn_W1_1", "L0_gnn_Wsc1"),
                                                        ("L1_gnn_W_l1_0", "L1_gnn_W_si0", "L1_gnn_W_l1_1", "L1_gnn_W_si1"))):
        arrays[f"node_s{n}"] = np.concatenate([a[s_msg], a[s_self]], 1)
        arrays[f"node_v{n}"] = np.concatenate([per_component(a[v_msg]), per_component(a[v_self])], 1)
    arrays["mlp_in0"] = np.zeros((PAIR * REC, PAIR * NH0), f)
    arrays["mlp_mid0"] = np.zeros((PAIR * NH0, PAIR * NH0), f)
    arrays["mlp_in1"] = np.zeros((PAIR * REC, PAIR * NH1), f)
    for j in range(PAIR):
        arrays["mlp_in0"][j * REC:j * REC + NB0, j * NH0:(j + 1) * NH0] = a["L0_gnn_Wfc1"]
        arrays["mlp_mid0"][j * NH0:(j + 1) * NH0, j * NH0:(j + 1) * NH0] = a["L0_gnn_Wfc2"]
        arrays["mlp_in1"][j * REC + NB0:j * REC + NB0 + NB1, j * NH1:(j + 1) * NH1] = a["L1_gnn_W_fc1"]
    w3 = a["L0_gnn_Wfc3"]
    w3 = np.concatenate([w3[:, 0:160], w3[:, 192:224], w3[:, 160:192]], 1)
    arrays["mlp_out0"] = np.concatenate([np.pad(w3, ((0, 0), (224 * j, 224 * (PAIR - 1 - j)))) for j in range(PAIR)], 0)
    arrays["mlp_out1"] = a["L1_gnn_W_fc2"]
    arrays["out_s0"] = a["L0_gnn_W2_0"]
    arrays["out_v0"] = a["L0_gnn_W2_1"]
    arrays["out_s1"] = np.concatenate([a["L1_gnn_W_l2_00"], a["L1_gnn_W_l2_10"]], 0)
    arrays["out_v1"] = np.concatenate([a["L1_gnn_W_l2_01"], a["L1_gnn_W_l2_11"]], 0)
    arrays = {k: np.ascontiguousarray(v) for k, v in arrays.items()}

    nc = bacc.Bacc("TRN2", target_bir_lowering=False, num_devices=1)
    t_in = {k: nc.dram_tensor("in_" + k, v.shape, mybir.dt.from_np(v.dtype), kind="ExternalInput").ap()
            for k, v in arrays.items()}
    out = nc.dram_tensor("out", (N_NODES, D), F32, kind="ExternalOutput").ap()
    build(nc, t_in, out)
    r = run_bass_kernel_spmd(nc, [{"in_" + k: v for k, v in arrays.items()}], core_ids=[0])
    return r.results[0]["out"]
```

```python
from contextlib import ExitStack, nullcontext

import numpy as np

import concourse.bass as bass
import concourse.mybir as mybir
from concourse.alu_op_type import AluOpType as ALU

F32 = mybir.dt.float32
I32 = mybir.dt.int32
ACT = mybir.ActivationFunctionType
AX = mybir.AxisListType

P = 128
N_NODES = 3125
N_EDGES = 103125
MUL_S, MUL_V = 64, 32
D_VEC = 3 * MUL_V
D = MUL_S + D_VEC
TILES = -(-N_NODES // P)
NODES_PAD = TILES * P
GROUP = 5
PAIR = 2
STEP = PAIR * P
RING = 6
ROUNDS = -(-N_EDGES // (STEP * RING))
STEPS = ROUNDS * RING
EDGES_PAD = STEPS * STEP
NB0, NB1 = 8, 10
REC = NB0 + NB1 + 4
SH = NB0 + NB1
NH0, NH1 = 64, 100
BLOCK_EDGES_COLS = -(-N_EDGES // P)
LOCAL_ROUNDS = -(-(P * BLOCK_EDGES_COLS // STEP + TILES) // RING)
LOCAL_STEPS = LOCAL_ROUNDS * RING
SIGNS = 14
D_MID = 4 * 96
COPIES = 4
ACC_ROWS = NODES_PAD + P
EPS = 1e-5
BANK = 512
AVG = 0.25


def build(nc, t_in, out):
    ctx = ExitStack()
    with ctx:
        def sb(name, shape, dt=F32):
            return ctx.enter_context(nc.sbuf_tensor(name, shape, dt))

        semaphores = {}

        def sem(name):
            if name not in semaphores:
                semaphores[name] = ctx.enter_context(nc.semaphore(name))
            return semaphores[name]

        psum = ctx.enter_context(nc.psum_tensor("psum", [P, 8, BANK], F32))
        X = sb("X", [P, TILES, D])
        skip = sb("skip", [P, TILES, D])
        sums = sb("sums", [P, COPIES, TILES, D])
        stage = sb("stage", [P, GROUP, D])
        xT = sb("xT", [D_VEC, 2, 2 * P])
        table_rows = sb("table_rows", [P, GROUP, D])
        stat = sb("stat", [P, 6, TILES])
        moments = sb("moments", [P, TILES, 8])
        ident = sb("ident", [P, P])
        before_mask = sb("before_mask", [P, P])
        dump_row = sb("dump_row", [P, 1])
        dump_row_i = sb("dump_row_i", [P, 1], I32)
        node_vec = sb("node_vec", [P, TILES])
        gains = sb("gains", [P, D - 2 * MUL_V])
        rec = sb("rec", [P, RING, PAIR, REC])
        key = sb("key", [P, RING, PAIR, 2], I32)
        target = sb("target", [P, RING, PAIR])
        gath = sb("gath", [P, RING, PAIR, D])
        radial = sb("radial", [NB1, RING, STEP])
        recT = sb("recT", [PAIR * REC, 2, P])
        hidA = sb("hidA", [P, 2, PAIR * P])
        hidB = sb("hidB", [P, 2, P])
        outer = sb("outer", [P, PAIR, 3 * 192])
        sw = sb("sw", [P, PAIR, MUL_S])
        mid = sb("mid", [P, 2, PAIR, 480])
        midT = sb("midT", [P, 2, PAIR, 4, P])
        same = sb("same", [P, RING, PAIR, P])
        junk = sb("junk", [P, PAIR, P])
        before = sb("before", [P, RING, PAIR])
        dump = sb("dump", [P, RING, PAIR])
        dest = sb("dest", [P, RING, PAIR], I32)
        msg = sb("msg", [P, 2, PAIR, D])
        msg_sum = sb("msg_sum", [P, 2, PAIR, D])
        tile_sums = sums[:, :, :, :].rearrange("p c t d -> p (c t d)")[:, 0:32 * D_MID] \
            .rearrange("p (t m) -> p t m", m=D_MID)
        dst_i = sb("dst_i", [P, BLOCK_EDGES_COLS], I32)
        dst_next = sb("dst_next", [P, BLOCK_EDGES_COLS], I32)
        dst_f = sb("dst_f", [P, BLOCK_EDGES_COLS])
        spare_cols = sb("spare_cols", [P, 2, BLOCK_EDGES_COLS])
        thresholds = sb("thresholds", [P, TILES + 1])
        thresholds_i = sb("thresholds_i", [P, TILES + 1], I32)
        below = sb("below", [P, TILES + 1])
        out_of_order = sb("out_of_order", [P, 1])
        general = sb("general", [P, 1], I32)
        first_edge = sb("first_edge", [P, LOCAL_STEPS], I32)
        packed_tiles = sb("packed_tiles", [P, 2 * (LOCAL_ROUNDS + 1)], mybir.dt.int16)
        tile_base = sb("tile_base", [P, LOCAL_STEPS])
        node_iota = sb("node_iota", [P, P])
        one_hot = sb("one_hot", [P, 2, PAIR, P])
        local = sb("local", [P, 2, PAIR])
        w = {k: sb("w_" + k, list(t_in[k].shape)) for k in WEIGHTS}

        table = [nc.dram_tensor(f"table{n}", [NODES_PAD, D], F32, kind="Internal").ap() for n in range(2)]
        acc = [[nc.dram_tensor(f"acc{n}_{c}", [ACC_ROWS, D], F32, kind="Internal").ap() for c in range(COPIES)]
               for n in range(2)]

        loaded, zeroed, dst_loaded = sem("loaded"), sem("zeroed"), sem("dst_loaded")
        targets_f, counted, signs_counted = sem("targets_f"), sem("counted"), sem("signs_counted")
        const, scaled = sem("const"), sem("scaled")
        with nc.Block() as block:
            @block.sync
            def _(sp):
                rows = P * BLOCK_EDGES_COLS
                sp.dma_start(dst_i[:, :], t_in["dst"][0:rows].rearrange("(p i) -> p i", p=P)).then_inc(dst_loaded, 16)
                sp.dma_start(dst_next[:, :], t_in["dst"][1:rows + 1].rearrange("(p i) -> p i", p=P)).then_inc(dst_loaded, 16)
                sp.dma_start(X[:, :, :], t_in["x"].rearrange("(t p) d -> p t d", p=P)).then_inc(loaded, 16)
                sp.dma_start(node_vec[:, :], t_in["node_vec"]).then_inc(loaded, 16)
                sp.dma_start(gains[:, :], t_in["gains"].unsqueeze(0).broadcast_to([P, MUL_S + MUL_V])).then_inc(loaded, 16)
                for k in WEIGHTS:
                    sp.dma_start(w[k][:, :], t_in[k]).then_inc(loaded, 16)
                sp.wait_ge(loaded, 16 * (3 + len(WEIGHTS)))

            @block.gpsimd
            def _(pool):
                pool.memset(ident[:, :], 0.0).then_inc(const, 1)
                pool.memset(before_mask[:, :], 1.0).then_inc(const, 1)
                pool.iota(dump_row_i[:, :], pattern=[[0, 1]], base=NODES_PAD, channel_multiplier=1).then_inc(const, 1)
                pool.iota(thresholds_i[:, :], pattern=[[P, TILES + 1]], base=0, channel_multiplier=0).then_inc(const, 1)
                pool.wait_ge(const, 4)
                pool.affine_select(out=ident[:, :], in_=ident[:, :], compare_op=ALU.not_equal, fill=1.0, base=0,
                                   pattern=[[-1, P]], channel_multiplier=1).then_inc(const, 1)
                pool.affine_select(out=before_mask[:, :], in_=before_mask[:, :], compare_op=ALU.is_gt, fill=0.0,
                                   base=0, pattern=[[-1, P]], channel_multiplier=1).then_inc(const, 1)

            @block.vector
            def _(dve):
                dve.wait_ge(const, 6)
                dve.tensor_copy(dump_row[:, :], dump_row_i[:, :]).then_inc(const, 1)
                dve.tensor_scalar(thresholds[:, :], thresholds_i[:, :], -0.5, None, ALU.add).then_inc(const, 1)
                dve.memset(sums[:, 0, :, :], 0.0).then_inc(scaled, 1)
                dve.memset(sums[:, 1, 0, :], 0.0).then_inc(scaled, 1)
                dve.memset(below[:, 0:1], 0.0)
                dve.wait_ge(dst_loaded, 32)
                dve.tensor_copy(dst_f[:, :], dst_i[:, :]).then_inc(targets_f, 1)
                dve.tensor_tensor(spare_cols[:, 0, :], dst_i[:, :], dst_next[:, :], ALU.is_gt).then_inc(counted, 1)
                dve.wait_ge(counted, 1)
                dve.tensor_reduce(out_of_order[:, :], spare_cols[:, 0, :], AX.X, ALU.add).then_inc(counted, 1)
                dve.wait_ge(targets_f, 1)
                for b in range(1, SIGNS):
                    dve.wait_ge(counted, b + 1)
                    dve.tensor_scalar(spare_cols[:, 0, :], dst_f[:, :], float(P * b), 0.0, ALU.is_lt, ALU.add,
                                      accum_out=below[:, b:b + 1]).then_inc(counted, 1)
                dve.wait_ge(loaded, 16 * (3 + len(WEIGHTS)))
                for k, lo, hi, f in SCALES:
                    dve.tensor_scalar(w[k][lo:hi, :], w[k][lo:hi, :], f, None, ALU.mult).then_inc(scaled, 1)

            @block.scalar
            def _(act):
                act.wait_ge(targets_f, 1)
                act.wait_ge(const, 8)
                for b in range(SIGNS, TILES + 1):
                    if b > SIGNS:
                        act.wait_ge(signs_counted, b - SIGNS)
                    act.activation(spare_cols[:, 1, :], dst_f[:, :], ACT.Sign, bias=thresholds[:, b:b + 1], scale=-1.0,
                                   accum_out=below[:, b:b + 1]).then_inc(signs_counted, 1)
                act.wait_ge(scaled, 2)
                act.wait_ge(loaded, 16 * (3 + len(WEIGHTS)))
                zero_sums(act, sums, acc[0], zeroed)

        plan = plan_steps(sem, sb, psum, below, out_of_order, general, first_edge, packed_tiles, tile_base,
                          node_iota, before_mask)
        for layer in range(2):
            node_projection(nc, layer, sem, psum, X, skip, stage, xT, table_rows, ident, node_vec, w,
                            table[layer], tile_sums if layer == 1 else None)
            if layer == 1:
                edge_layer_sorted(nc, sem, psum, t_in, rec, key, gath, radial, hidA, outer, sw, mid, one_hot, local,
                                  general, first_edge, packed_tiles, tile_base, node_iota, ident, w, table[1], tile_sums)
                project_sums(nc, sem, psum, X, skip, midT[:, 0, :, :, :].rearrange("p j k e -> p (j k) e")[:, 0:6, :]
                             .rearrange("p (b k) e -> p b k e", b=2), moments, node_vec, general, ident, w, tile_sums)
            edge_layer(nc, layer, sem, psum, t_in, rec, key, target, gath, recT, hidA, hidB, outer, sw, mid, midT,
                       same, junk, before, dump, dest, msg, msg_sum, before_mask, dump_row, ident, w,
                       table[layer], acc[layer], general if layer == 1 else None, zeroed, sums)
            finish_layer(nc, layer, sem, X, skip, sums, stat, moments, gains, node_vec, acc[layer], out,
                         general if layer == 1 else None, plan if layer == 0 else None)


def zero_sums(eng, sums, acc, zeroed):
    for c in range(COPIES):
        eng.dma_start(acc[c].rearrange("(p r) d -> p (r d)", p=P),
                      sums[:, 0:2, :, :].rearrange("p c t d -> p (c t d)")[:, 0:ACC_ROWS // P * D]).then_inc(zeroed, 16)


def plan_steps(sem, sb, psum, below, out_of_order, general, first_edge, packed_tiles, tile_base, node_iota,
               before_mask):
    T = TILES
    counted, planned, summed, taken = sem("p_counted"), sem("p_planned"), sem("p_summed"), sem("p_taken")
    ones = sb("ones", [P, 1])
    counts = sb("counts", [P, T])
    upto = sb("upto", [T, T])
    count, steps_i, steps, short, ends, d = (sb("p_" + k, [T, 1], I32 if k == "steps_i" else F32)
                                              for k in ("count", "steps_i", "steps", "short", "ends", "d"))
    wrong = sb("wrong", [1, 1])
    offsets = sb("offsets", [P, LOCAL_STEPS])
    iota_i = sb("iota_i", [P, LOCAL_STEPS], I32)
    tiles_f = sb("tiles_f", [P, LOCAL_ROUNDS + 1, 2, 3])
    halves = sb("halves", [P, LOCAL_ROUNDS + 1, 2])
    step_iota = sb("step_iota", [P, LOCAL_STEPS])
    ended = sb("ended", [T, LOCAL_STEPS])
    d_wide = sb("d_wide", [T, P])
    tile_wide = sb("tile_wide", [T, P])

    def pool_program(pool):
        n = [0]

        def step(ins):
            ins.then_inc(planned, 1)
            n[0] += 1
            pool.wait_ge(planned, n[0])

        pool.iota(iota_i[:, :], pattern=[[1, LOCAL_STEPS]], base=0, channel_multiplier=0)
        pool.memset(ones[:, :], 1.0)
        pool.memset(tile_wide[:, :], float(P))
        pool.memset(tiles_f[:, :, :, :], 0.0)
        step(pool.tensor_scalar(upto[:, :], before_mask[0:T, 0:T], -1.0, 1.0, ALU.mult, ALU.add))
        step(pool.tensor_copy(step_iota[:, :], iota_i[:, :]))
        pool.tensor_copy(node_iota[:, :], step_iota[:, 0:P])
        step(pool.tensor_scalar(below[:, SIGNS:T + 1], below[:, SIGNS:T + 1], float(BLOCK_EDGES_COLS), 0.5, ALU.add,
                                ALU.mult))
        step(pool.tensor_tensor(counts[:, :], below[:, 1:T + 1], below[:, 0:T], ALU.subtract))
        pool.sem_inc(counted, 1)
        pool.wait_ge(taken, 1)
        step(pool.tensor_scalar(general[0:1, :], wrong[:, :], 1.0, None, ALU.min))
        step(pool.tensor_scalar(steps_i[:, :], count[:, :], 1.0 / STEP, None, ALU.mult))
        step(pool.tensor_copy(steps[:, :], steps_i[:, :]))
        step(pool.tensor_scalar(short[:, :], steps[:, :], float(STEP), None, ALU.mult))
        step(pool.tensor_tensor(short[:, :], short[:, :], count[:, :], ALU.subtract))
        step(pool.tensor_scalar(short[:, :], short[:, :], 0.0, None, ALU.is_lt))
        step(pool.tensor_tensor(steps[:, :], steps[:, :], short[:, :], ALU.add))
        step(pool.tensor_scalar(d[:, :], steps[:, :], -float(STEP), None, ALU.mult))
        step(pool.tensor_tensor(d[:, :], d[:, :], count[:, :], ALU.add))
        step(pool.tensor_copy(d_wide[:, :], d[:, 0:1].broadcast_to([T, P])))
        pool.sem_inc(counted, 1)
        pool.wait_ge(taken, 2)
        step(pool.tensor_scalar(ended[:, :], step_iota[0:T, :], ends[:, 0:1], None, ALU.is_ge))
        pool.sem_inc(counted, 1)
        pool.wait_ge(taken, 4)
        step(pool.tensor_scalar(tiles_f[:, :, :, :].rearrange("p r h k -> p (r h k)")[:, 1:LOCAL_STEPS + 1],
                                tile_base[:, :], 1.0 / P, None, ALU.mult))
        step(pool.tensor_scalar(tiles_f[:, :, :, 1], tiles_f[:, :, :, 1], 32.0, None, ALU.mult))
        step(pool.tensor_scalar(tiles_f[:, :, :, 2], tiles_f[:, :, :, 2], 1024.0, None, ALU.mult))
        step(pool.tensor_tensor(halves[:, :, :], tiles_f[:, :, :, 0], tiles_f[:, :, :, 1], ALU.add))
        step(pool.tensor_tensor(halves[:, :, :], halves[:, :, :], tiles_f[:, :, :, 2], ALU.add))
        step(pool.tensor_copy(packed_tiles[:, :], halves[:, :, :].rearrange("p r h -> p (r h)")))
        step(pool.tensor_scalar(step_iota[:, :], step_iota[:, :], float(STEP), None, ALU.mult))
        step(pool.tensor_tensor(step_iota[:, :], step_iota[:, :], offsets[:, :], ALU.add))
        step(pool.tensor_scalar(first_edge[:, :], step_iota[:, :], float(N_EDGES), None, ALU.min))

    def tensor_program(pe):
        pe.wait_ge(counted, 1)
        pe.matmul(psum[0:T, 0, 0:1], counts[:, :], ones[:, :], start=True, stop=True)
        pe.matmul(psum[0:1, 0, 1:2], out_of_order[:, :], ones[:, :], start=True, stop=True).then_inc(summed, 1)
        pe.wait_ge(counted, 2)
        pe.matmul(psum[0:T, 1, 0:1], upto[:, :], steps[:, :], start=True, stop=True).then_inc(summed, 1)
        pe.wait_ge(counted, 3)
        pe.matmul(psum[:, 2, 0:LOCAL_STEPS], d_wide[:, :], ended[:, :], start=True, stop=True)
        pe.matmul(psum[:, 3, 0:LOCAL_STEPS], tile_wide[:, :], ended[:, :], start=True, stop=True).then_inc(summed, 1)

    def scalar_program(act):
        act.wait_ge(summed, 1)
        act.activation(count[:, :], psum[0:T, 0, 0:1], ACT.Copy)
        act.activation(wrong[:, :], psum[0:1, 0, 1:2], ACT.Copy).then_inc(taken, 1)
        act.wait_ge(summed, 2)
        act.activation(ends[:, :], psum[0:T, 1, 0:1], ACT.Copy).then_inc(taken, 1)
        act.wait_ge(summed, 3)
        act.activation(offsets[:, :], psum[:, 2, 0:LOCAL_STEPS], ACT.Copy).then_inc(taken, 1)
        act.activation(tile_base[:, :], psum[:, 3, 0:LOCAL_STEPS], ACT.Copy).then_inc(taken, 1)

    return {"pool": pool_program, "tensor": tensor_program, "scalar": scalar_program}


def edge_layer_sorted(nc, sem, psum, t_in, rec, key, gath, radial, hidA, outer, sw, mid, one_hot, local,
                      general, first_edge, packed_tiles, tile_base, node_iota, ident, w, table, tile_sums):
    gather_col, target_col = 0, 1
    mlp_in, mlp_out = w["radial_in1"], w["mlp_out1"]
    n_w = 192

    def name(what):
        return sem(f"e1_{what}")

    edges_loaded = [name(f"edges_loaded{u}") for u in range(RING)]
    gathered = [name(f"gathered{u}") for u in range(RING)]
    h_ready, hid_ready, w_ready = name("hA"), name("actA"), name("w")
    sw_ready, spread, ve_ready, we0_ready = name("sw"), name("spread"), name("ve"), name("we0")
    dot_ready, local_ready, mid_ready, added = name("dot"), name("local"), name("mid"), name("added")
    sum_psum, pool_turns = name("sum_psum"), name("pool_turns")

    ps_h = [psum[0:NH1, b, 0:PAIR * P] for b in (1, 6)]
    ps_w = [psum[:, b, 0:PAIR * n_w].rearrange("p (j n) -> p j n", j=PAIR) for b in (2, 3, 7)]
    ps_sum = [psum[:, 4 + b, 0:D_MID] for b in range(2)]
    S, ROUNDS_ = LOCAL_STEPS, LOCAL_ROUNDS

    def ahead(r, u, k):
        return r + (u + k) // RING, (u + k) % RING

    def exists(r, u):
        return not isinstance(r, int) or 0 <= RING * r + u < S

    def not_first(r, u, depth):
        return not isinstance(r, int) or RING * r + u >= depth

    def run(eng, turn):
        for r in (-1, 0):
            for u in range(RING):
                turn(r, u)
        with eng.Fori(1, ROUNDS_ - 1) as r:
            for u in range(RING):
                turn(r, u)
        for r in (ROUNDS_ - 1, ROUNDS_):
            for u in range(RING):
                turn(r, u)

    def wanted(eng):
        return eng.If(eng.value_load(general[0:1, 0:1], min_val=0, max_val=1) == 0)

    def by_row(columns):
        return columns.rearrange("k (p j) -> k p j", j=PAIR)

    def scalars(b):
        return mid[:, b, :, 0:96]

    def vectors(b):
        return mid[:, b, :, 96:D_MID].rearrange("p j (c n) -> p j c n", c=3)

    ve = outer[:, :, 0:D_VEC].rearrange("p j (c n) -> p j c n", c=3)
    dot = outer[:, :, D_VEC:D_VEC + MUL_V]
    we0 = [outer[:, :, 256 + 96 * b:256 + 96 * (b + 1)] for b in range(3)]

    packed_tiles = packed_tiles[:, :].bitcast(I32)
    with nc.Block() as block:
        @block.sync
        def _(sp):
            def load(r, u):
                s = RING * r + u
                if not_first(r, u, RING):
                    sp.wait_ge(mid_ready, s - RING + 1)
                    sp.wait_ge(spread, s - RING + 1)
                first = sp.value_load(first_edge[0:1, bass.ds(s, 1)], min_val=0, max_val=N_EDGES)
                sp.dma_start(radial[:, u, :], t_in["radial"][:, bass.ds(first, STEP)]).then_inc(edges_loaded[u], 16)
                sp.dma_start(rec[:, u, :, :].rearrange("p j f -> p (j f)"),
                             t_in["rec"][bass.ds(first, STEP), :].rearrange("(p j) f -> p (j f)", j=PAIR),
                             ).then_inc(edges_loaded[u], 16)
                sp.dma_start(key[:, u, :, :].rearrange("p j f -> p (j f)"),
                             t_in["keys"][bass.ds(first, STEP), :].rearrange("(p j) f -> p (j f)", j=PAIR),
                             ).then_inc(edges_loaded[u], 16)
            with wanted(sp):
                for u in range(RING):
                    load(0, u)
                with sp.Fori(1, ROUNDS_) as r:
                    for u in range(RING):
                        load(r, u)

        @block.gpsimd
        def _(pool):
            def gather(r, u):
                s = RING * r + u
                pool.wait_ge(edges_loaded[u], 48 * r + 48)
                if not_first(r, u, RING):
                    pool.wait_ge(mid_ready, s - RING + 1)
                pool.sem_inc(pool_turns, 1)
                for j in range(PAIR):
                    pool.indirect_dma_start(
                        gath[:, u, j, :], None, table,
                        bass.IndirectOffsetOnAxis(ap=key[:, u, j, gather_col:gather_col + 1], axis=0),
                    ).then_inc(gathered[u], 16)
            with wanted(pool):
                for u in range(RING):
                    gather(0, u)
                with pool.Fori(1, ROUNDS_) as r:
                    for u in range(RING):
                        gather(r, u)

        @block.tensor
        def _(pe):
            def hidden(r, u):
                s = RING * r + u
                if not_first(r, u, 2):
                    pe.wait_ge(hid_ready, s - 1)
                pe.wait_ge(edges_loaded[u], 48 * r + 48)
                pe.matmul(ps_h[u % 2], mlp_in[:, :], radial[:, u, :], start=True, stop=True).then_inc(h_ready, 1)

            def edge_weights(r, u):
                s = RING * r + u
                if not_first(r, u, 3):
                    pe.wait_ge(mid_ready, s - 2)
                pe.wait_ge(hid_ready, s + 1)
                for j in range(PAIR):
                    mm = pe.matmul(ps_w[u % 3][:, j, :], by_row(hidA[0:NH1, u % 2, :])[:, :, j], mlp_out[:, :],
                                   start=True, stop=True)
                mm.then_inc(w_ready, 1)

            def sum_targets(r, u):
                s = RING * r + u
                if not_first(r, u, 2):
                    pe.wait_ge(added, s - 1)
                pe.wait_ge(mid_ready, s + 1)
                pe.wait_ge(spread, s + 1)
                for j in range(PAIR):
                    mm = pe.matmul(ps_sum[u % 2], one_hot[:, u % 2, j, :], mid[:, u % 2, j, 0:D_MID],
                                   start=j == 0, stop=j == PAIR - 1)
                mm.then_inc(sum_psum, 1)

            def turn(r, u):
                if exists(*ahead(r, u, 4)):
                    hidden(*ahead(r, u, 4))
                if exists(*ahead(r, u, 3)):
                    edge_weights(*ahead(r, u, 3))
                if exists(r, u):
                    sum_targets(r, u)
            with wanted(pe):
                run(pe, turn)

        @block.scalar
        def _(act):
            def activate(r, u):
                s = RING * r + u
                if not_first(r, u, 2):
                    act.wait_ge(w_ready, s - 1)
                act.wait_ge(h_ready, s + 1)
                act.activation(hidA[0:NH1, u % 2, :], ps_h[u % 2], ACT.Relu, scale=NB1 ** -0.5).then_inc(hid_ready, 1)

            def spread_scalars(r, u):
                s = RING * r + u
                if not_first(r, u, 2):
                    act.wait_ge(sum_psum, s - 1)
                act.wait_ge(sw_ready, s + 1)
                for j in range(PAIR):
                    for c in range(3):
                        last = act.activation(mid[:, u % 2, j, 96 * (c + 1):96 * (c + 1) + MUL_S], sw[:, j, :], ACT.Copy,
                                              scale=rec[:, u, j, SH + c:SH + c + 1])
                last.then_inc(spread, 1)

            def scale_weights(r, u):
                s = RING * r + u
                if not_first(r, u, 3):
                    act.wait_ge(mid_ready, s - 2)
                act.wait_ge(w_ready, s + 1)
                for j in range(PAIR):
                    last = act.activation(we0[u % 3][:, j, :], ps_w[u % 3][:, j, 64:160], ACT.Copy, scale=rec[:, u, j, SH + 3:SH + 4])
                last.then_inc(we0_ready, 1)

            def turn(r, u):
                if exists(*ahead(r, u, 1)):
                    spread_scalars(*ahead(r, u, 1))
                if exists(*ahead(r, u, 3)):
                    scale_weights(*ahead(r, u, 3))
                if exists(*ahead(r, u, 4)):
                    activate(*ahead(r, u, 4))
            with wanted(act):
                run(act, turn)

        @block.vector
        def _(dve):
            packed = [None]

            def add_sums(r, u):
                s = RING * r + u
                k = (u + 1) % RING
                tile = (packed[0] >> (5 * (k % 3) + 16 * (k // 3))) & 31
                if not_first(r, u, 1):
                    dve.wait_ge(added, s)
                dve.wait_ge(sum_psum, s + 1)
                at = tile_sums[:, bass.ds(tile, 1), :].rearrange("p o m -> p (o m)")
                dve.tensor_tensor(at, ps_sum[u % 2], at, ALU.add).then_inc(added, 1)

            def turn(r, u):
                if u == 0 and (not isinstance(r, int) or r >= 0):
                    packed[0] = dve.value_load(packed_tiles[0:1, bass.ds(r, 1)], min_val=0, max_val=2 ** 31 - 1)
                a = ahead(r, u, 1)
                b = ahead(r, u, -1)
                if exists(*a):
                    ra, ua = a
                    s = RING * ra + ua
                    slot = ua % 2
                    scal = gath[:, ua, :, 0:MUL_S]
                    vec = gath[:, ua, :, MUL_S:D].rearrange("p j (c n) -> p j c n", c=3)
                    wt, mid_s, mid_v = ps_w[ua % 3], scalars(slot), vectors(slot)
                    dve.wait_ge(gathered[ua], 32 * ra + 32)
                    if not_first(ra, ua, 1):
                        dve.wait_ge(spread, s)
                    dve.wait_ge(we0_ready, s + 1)
                    dve.tensor_tensor(sw[:, :, :], wt[:, :, 0:64], scal, ALU.mult).then_inc(sw_ready, 1)
                    dve.tensor_tensor(local[:, slot, :], key[:, ua, :, target_col],
                                      tile_base[:, bass.ds(s, 1)].broadcast_to([P, PAIR]), ALU.subtract).then_inc(local_ready, 1)
                    dve.tensor_tensor(ve, vec, rec[:, ua, :, SH:SH + 3].unsqueeze(3).broadcast_to([P, PAIR, 3, MUL_V]),
                                      ALU.mult).then_inc(ve_ready, 1)
                if exists(*b):
                    add_sums(*b)
                if exists(*a):
                    dve.wait_ge(ve_ready, s + 1)
                    dve.tensor_reduce(dot, ve.rearrange("p j c n -> p j n c"), AX.X, ALU.add).then_inc(dot_ready, 1)
                    if not_first(ra, ua, 2):
                        dve.wait_ge(sum_psum, s - 1)
                    dve.tensor_tensor(mid_s[:, :, 0:MUL_S], we0[ua % 3][:, :, 0:MUL_S], scal, ALU.mult)
                    dve.wait_ge(local_ready, s + 1)
                    dve.tensor_tensor(one_hot[:, slot, :, :], node_iota[:, :].unsqueeze(1).broadcast_to([P, PAIR, P]),
                                      local[:, slot, :].unsqueeze(2).broadcast_to([P, PAIR, P]), ALU.is_equal)
                    dve.wait_ge(dot_ready, s + 1)
                    dve.tensor_tensor(mid_s[:, :, MUL_S:96], wt[:, :, 160:192], dot, ALU.mult)
                    dve.tensor_tensor(mid_v[:, :, :, 64:96], vec, we0[ua % 3][:, :, MUL_S:96].unsqueeze(2)
                                      .broadcast_to([P, PAIR, 3, MUL_V]), ALU.mult).then_inc(mid_ready, 1)
            with wanted(dve):
                run(dve, turn)


def residual(dve, t, X, skip, node_vec, mixed):
    scal, vec = slice(0, MUL_S), slice(MUL_S, D)
    dve.scalar_tensor_tensor(X[:, t, scal], skip[:, t, scal], node_vec[:, t:t + 1], X[:, t, scal], ALU.mult, ALU.add)
    xv = X[:, t, vec].rearrange("p (n c) -> p n c", c=3)
    dve.scalar_tensor_tensor(xv, skip[:, t, vec].rearrange("p (c n) -> p n c", c=3), node_vec[:, t:t + 1], xv,
                             ALU.mult, ALU.add).then_inc(mixed, 1)


def project_sums(nc, sem, psum, X, skip, sums_T, moments, node_vec, general, ident, w, tile_sums):
    turned, taken, projected, summed = (sem(f"q_{k}") for k in ("turned", "taken", "projected", "summed"))
    mixed, measured = sem("f1_mixed"), sem("f1_measured")
    chunks = D_MID // P

    def wanted(eng):
        return eng.If(eng.value_load(general[0:1, 0:1], min_val=0, max_val=1) == 0)

    with nc.Block() as block:
        @block.tensor
        def _(pe):
            def turn(t):
                if t >= 2:
                    pe.wait_ge(taken, t - 1)
                for k in range(chunks):
                    mm = pe.transpose(psum[:, t % 2, k * P:(k + 1) * P], tile_sums[:, t, k * P:(k + 1) * P], ident[:, :])
                mm.then_inc(turned, 1)

            def project(t):
                if t >= 2:
                    pe.wait_ge(summed, t - 1)
                pe.wait_ge(taken, t + 1)
                for k in range(chunks):
                    mm = pe.matmul(psum[:, 2 + t % 2, 0:D], sums_T[:, t % 2, k, :], w[f"out1_{k}"][:, :],
                                   start=k == 0, stop=k == chunks - 1)
                mm.then_inc(projected, 1)

            with wanted(pe):
                for t in range(TILES + 1):
                    if t < TILES:
                        turn(t)
                    if t >= 1:
                        project(t - 1)

        @block.scalar
        def _(act):
            with wanted(act):
                for t in range(TILES):
                    if t >= 2:
                        act.wait_ge(projected, t - 1)
                    act.wait_ge(turned, t + 1)
                    act.activation(sums_T[:, t % 2, :, :].rearrange("p k e -> p (k e)"), psum[:, t % 2, 0:D_MID],
                                   ACT.Copy).then_inc(taken, 1)

        @block.vector
        def _(dve):
            with wanted(dve):
                for t in range(TILES + 2):
                    if t < TILES:
                        dve.wait_ge(projected, t + 1)
                        dve.tensor_tensor(skip[:, t, :], psum[:, 2 + t % 2, 0:D], skip[:, t, :], ALU.add).then_inc(summed, 1)
                    if 2 <= t:
                        dve.wait_ge(mixed, t - 1)
                        dve.bn_stats(moments[:, t - 2, 0:6], X[:, t - 2, :]).then_inc(measured, 1)
                    if 1 <= t <= TILES:
                        dve.wait_ge(summed, t)
                        residual(dve, t - 1, X, skip, node_vec, mixed)


def node_projection(nc, layer, sem, psum, X, skip, stage, xT, table_rows, ident, node_vec, w, table,
                    tile_sums=None):
    def name(what):
        return sem(f"n{layer}_{what}")

    staged, turned, xT_ready, projected = name("staged"), name("turned"), name("xT"), name("projected")
    rows_ready, skip_ready = name("rows"), name("skip")
    stored = [name(f"stored{k}") for k in range(GROUP)]
    ws = w[f"node_s{layer}"][:, :].rearrange("k (h n) -> k h n", h=2)
    wv = w[f"node_v{layer}"][:, :].rearrange("k (h n) -> k h n", h=2)
    results = [psum[:, 2 + k, 0:2 * D].rearrange("p (h d) -> p h d", h=2) for k in range(GROUP)]
    groups = TILES // GROUP
    table_v = table.rearrange("(t p) d -> p t d", p=P)

    def run(eng, body):
        body(0)
        with eng.Fori(1, groups) as g:
            body(g)

    with nc.Block() as block:
        @block.vector
        def _(dve):
            def copy_tile(g, k):
                dve.tensor_copy(stage[:, k, :], X[:, bass.ds(g * GROUP + k, 1), :].rearrange("p o d -> p (o d)")).then_inc(staged, 1)

            def body(g, last=False):
                for k in range(GROUP):
                    t = g * GROUP + k
                    if not last:
                        dve.wait_ge(turned, t + 1)
                        copy_tile(g + 1, k)
                    dve.wait_ge(rows_ready if layer == 0 else projected, t + 1)
                    if layer == 1:
                        if not isinstance(g, int) or g > 0:
                            dve.wait_ge(stored[k], 16 * g)
                        dve.tensor_tensor(table_rows[:, k, :], results[k][:, 0, :],
                                          node_vec[:, bass.ds(t, 1)].broadcast_to([P, D]), ALU.mult).then_inc(rows_ready, 1)
                    dve.tensor_copy(skip[:, bass.ds(t, 1), :].rearrange("p o d -> p (o d)"),
                                    results[k][:, 1, :]).then_inc(skip_ready, 1)

            for k in range(GROUP):
                copy_tile(0, k)
            body(0)
            with dve.Fori(1, groups - 1) as g:
                body(g)
            body(groups - 1, last=True)

        @block.tensor
        def _(pe):
            def body(g):
                later = not isinstance(g, int)
                def turn(k):
                    pe.wait_ge(staged, g * GROUP + k + 1)
                    for half, lo in enumerate((0, MUL_S)):
                        mm = pe.transpose(psum[0:D_VEC, k % 2, half * P:(half + 1) * P], stage[:, k, lo:lo + D_VEC], ident[:, :])
                    mm.then_inc(turned, 1)

                def project(k):
                    t = g * GROUP + k
                    if later:
                        pe.wait_ge(skip_ready, t + 1 - GROUP)
                    pe.wait_ge(xT_ready, t + 1)
                    pe.matmul(results[k][:, :, 0:MUL_S], xT[0:MUL_S, k % 2, 0:P], ws, start=True, stop=True)
                    pe.matmul(results[k][:, :, MUL_S:D], xT[:, k % 2, P:2 * P], wv, start=True, stop=True).then_inc(projected, 1)

                if later:
                    pe.wait_ge(xT_ready, g * GROUP)
                turn(0)
                turn(1)
                for k in range(GROUP):
                    project(k)
                    if k + 2 < GROUP:
                        turn(k + 2)
            run(pe, body)

        @block.scalar
        def _(act):
            def body(g):
                later = not isinstance(g, int)
                def take(k):
                    t = g * GROUP + k
                    act.wait_ge(turned, t + 1)
                    if k >= 2:
                        act.wait_ge(projected, t - 1)
                    act.activation(xT[:, k % 2, :], psum[0:D_VEC, k % 2, 0:2 * P], ACT.Copy).then_inc(xT_ready, 1)

                if later:
                    act.wait_ge(projected, g * GROUP)
                take(0)
                take(1)
                for k in range(GROUP):
                    if layer == 0:
                        act.wait_ge(projected, g * GROUP + k + 1)
                        if later:
                            act.wait_ge(stored[k], 16 * g)
                        act.activation(table_rows[:, k, :], results[k][:, 0, :], ACT.Copy).then_inc(rows_ready, 1)
                    if k + 2 < GROUP:
                        take(k + 2)
            run(act, body)

        @block.sync
        def _(sp):
            def body(g):
                later = not isinstance(g, int)
                for k in range(GROUP):
                    sp.wait_ge(rows_ready, g * GROUP + k + 1)
                    sp.dma_start(table_v[:, bass.ds(g * GROUP + k, 1), :].rearrange("p o d -> p (o d)"),
                                 table_rows[:, k, :]).then_inc(stored[k], 16)
            run(sp, body)
            for k in range(GROUP):
                sp.wait_ge(stored[k], 16 * groups)

        if tile_sums is not None:
            @block.gpsimd
            def _(pool):
                pool.memset(tile_sums[:, 0:TILES + 1, :], 0.0)


def edge_layer(nc, layer, sem, psum, t_in, rec, key, target, gath, recT, hidA, hidB, outer, sw, mid, midT,
               same, junk, before, dump, dest, msg, msg_sum, before_mask, dump_row, ident, w, table, acc, general, zeroed,
               sums):
    L0 = layer == 0
    gather_col, scatter_col = (1, 0) if L0 else (0, 1)
    hidden = NH0 if L0 else NH1
    n_w = 224 if L0 else 192
    chunks = [(0, 128), (224, 128), (128, 96)] if L0 else [(96 * k, 96) for k in range(4)]
    n_mid = 352 if L0 else 384
    w0, w1 = (0, 64) if L0 else (64, 0)
    PARTS = 12 if L0 else 9
    mlp_in, mlp_out = w[f"mlp_in{layer}"], w[f"mlp_out{layer}"]
    rows_v = t_in["rec"].rearrange("(s p j) f -> s p (j f)", p=P, j=PAIR)
    keys_v = t_in["keys"].rearrange("(s p j) f -> s p (j f)", p=P, j=PAIR)

    def name(what):
        return sem(f"e{layer}_{what}")

    edges_loaded = [name(f"edges_loaded{u}") for u in range(RING)]
    gathered = [name(f"gathered{u}") for u in range(RING)]
    scattered = [name(f"scattered{c}") for c in range(COPIES)]
    target_ready, turned, recT_ready = name("target_ready"), name("turned"), name("recT_ready")
    hA_ready, actA_ready, hB_ready, actB_ready = name("hA"), name("actA"), name("hB"), name("actB")
    w_ready, midT_psum, midT_ready = name("w"), name("midT_psum"), name("midT")
    msg_psum, msg_ready, sum_psum, sum_ready = name("msg_psum"), name("msg"), name("sum_psum"), name("sum")
    same_ready, before_ready, dump_ready, dest_ready = name("same"), name("before"), name("dump"), name("dest")
    pool_zeros, acc_zeroed = name("pool_zeros"), name("acc_zeroed")
    msg_spread = name("msg_spread")
    part = name("part")
    pool_turns = name("pool_turns")

    ps_turn = psum[:, 0, :]
    ps_hA = psum[:, 1, 0:PAIR * P]
    ps_hB = psum[:, 1, PAIR * P:PAIR * P + P]
    ps_w = [psum[:, 2 + b, 0:PAIR * n_w].rearrange("p (j n) -> p j n", j=PAIR) for b in range(2)]
    ps_mid = [psum[:, 4 + j, :].rearrange("p (k e) -> p k e", k=4) for j in range(PAIR)]
    ps_msg = psum[:, 6, 0:PAIR * (D + MUL_V if L0 else D)].rearrange("p (j d) -> p j d", j=PAIR)
    ps_sum = psum[:, 7, 0:PAIR * D].rearrange("p (j d) -> p j d", j=PAIR)

    def ahead(r, u, k):
        return r + (u + k) // RING, (u + k) % RING

    def exists(r, u):
        return not isinstance(r, int) or 0 <= RING * r + u < STEPS

    def not_first(r, u, depth):
        return not isinstance(r, int) or RING * r + u >= depth

    def uses(r, u):
        return RING // 2 * r + u // 2

    def run(eng, turn):
        for r in (-1, 0):
            for u in range(RING):
                turn(r, u)
        with eng.Fori(1, ROUNDS - 1) as r:
            for u in range(RING):
                turn(r, u)
        for r in (ROUNDS - 1, ROUNDS):
            for u in range(RING):
                turn(r, u)

    def wanted(eng):
        return nullcontext() if general is None else eng.If(eng.value_load(general[0:1, 0:1], min_val=0, max_val=1) == 1)

    def scalars(b):
        return mid[:, b, :, 0:96]

    def vectors(b):
        return mid[:, b, :, 160 if L0 else 96:n_mid].rearrange("p j (c n) -> p j c n", c=3)

    with nc.Block() as block:
        @block.sync
        def _(sp):
            def load(r, u):
                s = RING * r + u
                if not_first(r, u, RING):
                    if L0:
                        sp.wait_ge(msg_ready, s - RING + 1)
                    else:
                        sp.wait_ge(part, PARTS * (s - RING + 1))
                sp.dma_start(rec[:, u, :, :].rearrange("p j f -> p (j f)"),
                             rows_v[bass.ds(s, 1), :, :].rearrange("s p f -> (s p) f")).then_inc(edges_loaded[u], 16)
                sp.dma_start(key[:, u, :, :].rearrange("p j f -> p (j f)"),
                             keys_v[bass.ds(s, 1), :, :].rearrange("s p f -> (s p) f")).then_inc(edges_loaded[u], 16)
            with wanted(sp):
                for u in range(RING):
                    load(0, u)
                with sp.Fori(1, ROUNDS) as r:
                    for u in range(RING):
                        load(r, u)

        @block.gpsimd
        def _(pool):
            def gather(r, u):
                s = RING * r + u
                pool.wait_ge(edges_loaded[u], 32 * r + 32)
                if not_first(r, u, RING):
                    pool.wait_ge(part, PARTS * (s - RING + 1))
                pool.sem_inc(pool_turns, 1)
                for j in range(PAIR):
                    pool.indirect_dma_start(
                        gath[:, u, j, :], None, table,
                        bass.IndirectOffsetOnAxis(ap=key[:, u, j, gather_col:gather_col + 1], axis=0),
                    ).then_inc(gathered[u], 16)

            def scatter(r, u):
                s = RING * r + u
                pool.wait_ge(sum_ready, s + 1)
                pool.wait_ge(dest_ready, s + 1)
                for j in range(PAIR):
                    c = PAIR * (u % 2) + j
                    if not_first(r, u, 2):
                        pool.wait_ge(scattered[c], 16 * uses(r, u))
                pool.sem_inc(pool_turns, 1)
                for j in range(PAIR):
                    c = PAIR * (u % 2) + j
                    pool.indirect_dma_start(
                        acc[c], bass.IndirectOffsetOnAxis(ap=dest[:, u, j:j + 1], axis=0),
                        msg_sum[:, u % 2, j, :], None, compute_op=ALU.add,
                    ).then_inc(scattered[c], 16)

            def turn(r, u):
                if exists(*ahead(r, u, 3)):
                    gather(*ahead(r, u, 3))
                if exists(*ahead(r, u, -3)):
                    scatter(*ahead(r, u, -3))
            with wanted(pool):
                if L0:
                    pool.wait_ge(zeroed, 16 * COPIES)
                else:
                    pool.memset(sums[:, 0, :, :], 0.0).then_inc(pool_zeros, 1)
                    pool.memset(sums[:, 1, 0, :], 0.0).then_inc(pool_zeros, 1)
                    pool.wait_ge(pool_zeros, 2)
                    zero_sums(pool, sums, acc, acc_zeroed)
                    pool.wait_ge(acc_zeroed, 16 * COPIES)
                run(pool, turn)
                for c in range(COPIES):
                    pool.wait_ge(scattered[c], 16 * STEPS // 2)

        @block.tensor
        def _(pe):
            def turn_edges(r, u):
                s = RING * r + u
                pe.wait_ge(edges_loaded[u], 32 * r + 32)
                if not_first(r, u, 1):
                    pe.wait_ge(same_ready, s)
                pe.wait_ge(target_ready, s + 1)
                for j in range(PAIR):
                    pe.transpose(ps_turn[:, P * (1 + j):P * (2 + j)], target[:, u, j:j + 1].broadcast_to([P, P]),
                                 ident[:, :])
                mm = pe.transpose(ps_turn[0:PAIR * REC, 0:P], rec[:, u, :, :].rearrange("p j f -> p (j f)"), ident[:, :])
                mm.then_inc(turned, 1)

            def hidden_a(r, u):
                s = RING * r + u
                if not_first(r, u, 1):
                    pe.wait_ge(actB_ready if L0 else actA_ready, s)
                pe.wait_ge(recT_ready, s + 1)
                if L0:
                    mm = pe.matmul(ps_hA[:, 0:P], mlp_in[:, :], recT[:, u % 2, :], start=True, stop=True)
                else:
                    for j in range(PAIR):
                        mm = pe.matmul(ps_hA[0:NH1, j * P:(j + 1) * P], mlp_in[:, j * NH1:(j + 1) * NH1],
                                       recT[:, u % 2, :], start=True, stop=True)
                mm.then_inc(hA_ready, 1)

            def hidden_b(r, u):
                s = RING * r + u
                pe.wait_ge(actA_ready, s + 1)
                pe.matmul(ps_hB, w["mlp_mid0"][:, :], hidA[:, u % 2, 0:P], start=True, stop=True).then_inc(hB_ready, 1)

            def edge_weights(r, u):
                s = RING * r + u
                if not_first(r, u, 2):
                    pe.wait_ge(part, PARTS * (s - 1))
                pe.wait_ge(actB_ready if L0 else actA_ready, s + 1)
                if L0:
                    mm = pe.matmul(ps_w[u % 2].rearrange("p j n -> p (j n)"), hidB[:, u % 2, :], mlp_out[:, :],
                                   start=True, stop=True)
                else:
                    for j in range(PAIR):
                        mm = pe.matmul(ps_w[u % 2][:, j, :], hidA[0:NH1, u % 2, j * P:(j + 1) * P], mlp_out[:, :],
                                       start=True, stop=True)
                mm.then_inc(w_ready, 1)

            def turn_messages(r, u):
                s = RING * r + u
                if not_first(r, u, 1):
                    pe.wait_ge(midT_ready, 2 * s)
                pe.wait_ge(part, PARTS * (s + 1))
                for j in range(PAIR):
                    for k, (start, width) in enumerate(chunks):
                        mm = pe.transpose(ps_mid[j][0:width, k, :], mid[:, u % 2, j, start:start + width], ident[:, :])
                    mm.then_inc(midT_psum, 1)

            def project(r, u):
                s = RING * r + u
                if not_first(r, u, 1):
                    pe.wait_ge(msg_ready, s)
                for j in range(PAIR):
                    pe.wait_ge(midT_ready, 2 * s + j + 1)
                    if L0:
                        pe.matmul(ps_msg[:, j, 0:128], midT[:, u % 2, j, 0, :], w["out_first0"][:, :], start=True, stop=False)
                        pe.matmul(ps_msg[:, j, 32:128], midT[0:96, u % 2, j, 2, :], w["out_last0"][:, :], start=False, stop=True)
                        mm = pe.matmul(ps_msg[:, j, 128:192], midT[:, u % 2, j, 1, :], w["out_mid0"][:, :], start=True, stop=True)
                    else:
                        pe.matmul(ps_msg[:, j, 0:MUL_S], midT[0:96, u % 2, j, 0, :], w["out_s1"][:, :], start=True, stop=True)
                        for c in range(3):
                            mm = pe.matmul(ps_msg[:, j, MUL_S + c * MUL_V:MUL_S + (c + 1) * MUL_V],
                                           midT[0:96, u % 2, j, 1 + c, :], w["out_v1"][:, :], start=True, stop=True)
                mm.then_inc(msg_psum, 1)

            def sum_same(r, u):
                s = RING * r + u
                if not_first(r, u, 1):
                    pe.wait_ge(sum_ready, s)
                pe.wait_ge(msg_ready, s + 1)
                for j in range(PAIR):
                    mm = pe.matmul(ps_sum[:, j, :], same[:, u, j, :], msg[:, u % 2, j, :], start=True, stop=True)
                mm.then_inc(sum_psum, 1)

            def turn(r, u):
                if exists(*ahead(r, u, 2)):
                    hidden_a(*ahead(r, u, 2))
                if exists(*ahead(r, u, -1)):
                    project(*ahead(r, u, -1))
                if exists(*ahead(r, u, 3)):
                    turn_edges(*ahead(r, u, 3))
                if L0 and exists(*ahead(r, u, 2)):
                    hidden_b(*ahead(r, u, 2))
                if exists(r, u):
                    turn_messages(r, u)
                if exists(*ahead(r, u, -2)):
                    sum_same(*ahead(r, u, -2))
                if exists(*ahead(r, u, 2)):
                    edge_weights(*ahead(r, u, 2))
            with wanted(pe):
                run(pe, turn)

        @block.scalar
        def _(act):
            def targets(r, u):
                s = RING * r + u
                act.wait_ge(edges_loaded[u], 32 * r + 32)
                if not_first(r, u, RING):
                    act.wait_ge(dest_ready, s - RING + 1)
                act.activation(target[:, u, :], key[:, u, :, scatter_col], ACT.Copy).then_inc(target_ready, 1)

            def take_turned(r, u):
                s = RING * r + u
                act.wait_ge(turned, s + 1)
                if not_first(r, u, 2):
                    act.wait_ge(hA_ready, s - 1)
                act.activation(recT[:, u % 2, :], ps_turn[0:PAIR * REC, 0:P], ACT.Copy).then_inc(recT_ready, 1)

            def activate_a(r, u):
                s = RING * r + u
                act.wait_ge(hA_ready, s + 1)
                if not_first(r, u, 2):
                    act.wait_ge(hB_ready if L0 else w_ready, s - 1)
                if L0:
                    act.activation(hidA[:, u % 2, 0:P], ps_hA[:, 0:P], ACT.Silu, scale=NB0 ** -0.5).then_inc(actA_ready, 1)
                else:
                    act.activation(hidA[0:NH1, u % 2, :], ps_hA[0:NH1, :], ACT.Relu,
                                   scale=NB1 ** -0.5).then_inc(actA_ready, 1)

            def activate_b(r, u):
                s = RING * r + u
                act.wait_ge(hB_ready, s + 1)
                if not_first(r, u, 2):
                    act.wait_ge(w_ready, s - 1)
                act.activation(hidB[:, u % 2, :], ps_hB, ACT.Silu, scale=NH0 ** -0.5).then_inc(actB_ready, 1)

            def take_mid(r, u, j):
                s = RING * r + u
                act.wait_ge(midT_psum, 2 * s + j + 1)
                if not_first(r, u, 2):
                    act.wait_ge(msg_psum, s - 1)
                if L0:
                    act.activation(midT[:, u % 2, j, 0:2, :], ps_mid[j][:, 0:2, :], ACT.Copy)
                    act.activation(midT[0:96, u % 2, j, 2, :], ps_mid[j][0:96, 2, :], ACT.Copy).then_inc(midT_ready, 1)
                else:
                    act.activation(midT[0:96, u % 2, j, :, :], ps_mid[j][0:96, :, :], ACT.Copy).then_inc(midT_ready, 1)

            def take_msg(r, u):
                s = RING * r + u
                act.wait_ge(msg_psum, s + 1)
                if not_first(r, u, 2):
                    act.wait_ge(sum_psum, s - 1)
                if L0:
                    act.activation(msg[:, u % 2, :, 0:MUL_S], ps_msg[:, :, 32:96], ACT.Copy)
                    for j in range(PAIR):
                        for c in range(3):
                            last = act.activation(msg[:, u % 2, j, MUL_S + c * MUL_V:MUL_S + (c + 1) * MUL_V],
                                                  ps_msg[:, j, 0:MUL_V], ACT.Copy, scale=rec[:, u, j, SH + c:SH + c + 1])
                    last.then_inc(msg_spread, 1)
                else:
                    act.activation(msg[:, u % 2, :, :], ps_msg, ACT.Copy).then_inc(msg_ready, 1)

            def take_sum(r, u):
                s = RING * r + u
                for j in range(PAIR):
                    c = PAIR * (u % 2) + j
                    if not_first(r, u, 2):
                        act.wait_ge(scattered[c], 16 * uses(r, u))
                act.wait_ge(sum_psum, s + 1)
                act.activation(msg_sum[:, u % 2, :, :], ps_sum, ACT.Copy).then_inc(sum_ready, 1)

            def turn(r, u):
                if exists(*ahead(r, u, 2)):
                    activate_a(*ahead(r, u, 2))
                if exists(*ahead(r, u, -3)):
                    take_sum(*ahead(r, u, -3))
                if exists(*ahead(r, u, -1)):
                    take_msg(*ahead(r, u, -1))
                if L0 and exists(*ahead(r, u, 2)):
                    activate_b(*ahead(r, u, 2))
                for j in range(PAIR):
                    if exists(r, u):
                        take_mid(r, u, j)
                if exists(*ahead(r, u, 3)):
                    take_turned(*ahead(r, u, 3))
                if exists(*ahead(r, u, 4)):
                    targets(*ahead(r, u, 4))
            with wanted(act):
                run(act, turn)

        @block.vector
        def _(dve):
            def same_targets(r, u):
                s = RING * r + u
                dve.wait_ge(recT_ready, s + 1)
                if not_first(r, u, RING):
                    dve.wait_ge(sum_psum, s - RING + 1)
                dve.tensor_tensor(same[:, u, :, :], ps_turn[:, P:3 * P].rearrange("p (j e) -> p j e", j=PAIR),
                                  target[:, u, :].unsqueeze(2).broadcast_to([P, PAIR, P]),
                                  ALU.is_equal).then_inc(same_ready, 1)

            def count_before(r, u):
                s = RING * r + u
                dve.wait_ge(same_ready, s + 1)
                if not_first(r, u, 1):
                    dve.wait_ge(before_ready, 2 * s)
                for j in range(PAIR):
                    dve.scalar_tensor_tensor(junk[:, j, :], same[:, u, j, :], 1.0, before_mask[:, :], ALU.mult, ALU.mult,
                                             accum_out=before[:, u, j:j + 1]).then_inc(before_ready, 1)

            def dump_rows(r, u):
                s = RING * r + u
                dve.wait_ge(before_ready, 2 * s + 2)
                dve.tensor_scalar(dump[:, u, :], before[:, u, :], 1.0, dump_row[:, 0:1], ALU.min,
                                  ALU.mult).then_inc(dump_ready, 1)

            def destinations(r, u):
                s = RING * r + u
                for j in range(PAIR):
                    if not_first(r, u, RING):
                        dve.wait_ge(scattered[PAIR * (u % 2) + j], 16 * (uses(r, u) - RING // 2 + 1))
                dve.wait_ge(dump_ready, s + 1)
                dve.tensor_tensor(dest[:, u, :], dump[:, u, :], target[:, u, :], ALU.max).then_inc(dest_ready, 1)

            def views(r, u):
                b = u % 2
                scal, vec = gath[:, u, :, 0:MUL_S], gath[:, u, :, MUL_S:D].rearrange("p j (a n) -> p j a n", a=3)
                return scal, vec, rec[:, u, :, SH:SH + 4], ps_w[b], scalars(b), vectors(b)

            def weighted_scalars(r, u):
                s = RING * r + u
                scal, _, sh, wt, mid_s, _ = views(r, u)
                if not_first(r, u, 2):
                    dve.wait_ge(midT_psum, 2 * s - 2)
                dve.wait_ge(w_ready, s + 1)
                w1_s = mid[:, u % 2, :, 64:128] if L0 else sw[:, :, :]
                dve.tensor_tensor(w1_s, wt[:, :, w1:w1 + 64], scal, ALU.mult).then_inc(part, 1)
                for j in range(PAIR):
                    dve.scalar_tensor_tensor(mid_s[:, j, 0:MUL_S], wt[:, j, w0:w0 + 64], sh[:, j, 3:4], scal[:, j, :],
                                             ALU.mult, ALU.mult).then_inc(part, 1)

            def spread_scalars(r, u):
                _, _, sh, _, _, mid_v = views(r, u)
                dve.tensor_tensor(mid_v[:, :, :, 0:64], sw[:, :, :].unsqueeze(2).broadcast_to([P, PAIR, 3, 64]),
                                  sh[:, :, 0:3].unsqueeze(3).broadcast_to([P, PAIR, 3, 64]),
                                  ALU.mult).then_inc(part, 1)

            def add_components(r, u):
                s = RING * r + u
                dve.wait_ge(msg_spread, s + 1)
                dve.tensor_tensor(msg[:, u % 2, :, MUL_S:D], ps_msg[:, :, 96:192], msg[:, u % 2, :, MUL_S:D],
                                  ALU.add).then_inc(msg_ready, 1)

            def turn_0(a, b):
                slots = outer[:, :, 0:480].rearrange("p j (a b n) -> p j a b n", a=3, b=5)
                flat = outer[:, :, 0:480].rearrange("p j (q n) -> p j q n", n=MUL_V)
                trace = outer[:, :, :].rearrange("p j (a m) -> p j a m", a=3)[:, :, :, 0:MUL_V]
                if b:
                    same_targets(*b)
                if a:
                    r, u = a
                    s = RING * r + u
                    done = PARTS * s
                    _, vec, sh, wt, mid_s, mid_v = views(r, u)
                    dve.wait_ge(edges_loaded[u], 32 * r + 32)
                    dve.wait_ge(gathered[u], 32 * r + 32)
                    if not_first(r, u, 1):
                        dve.wait_ge(part, done)
                    for j in range(PAIR):
                        dve.tensor_tensor(slots[:, j, :, 0:4, :],
                                          vec[:, j, :, :].unsqueeze(2).broadcast_to([P, 3, 4, MUL_V]),
                                          sh[:, j, :].unsqueeze(1).unsqueeze(3).broadcast_to([P, 3, 4, MUL_V]),
                                          ALU.mult).then_inc(part, 1)
                if b:
                    count_before(*b)
                if a:
                    dve.wait_ge(part, done + 2)
                    for c in range(3):
                        a1, a2 = (c + 1) % 3, (c + 2) % 3
                        dve.tensor_tensor(flat[:, :, 5 * c + 4, :], flat[:, :, 5 * a1 + a2, :],
                                          flat[:, :, 5 * a2 + a1, :], ALU.subtract).then_inc(part, 1)
                    weighted_scalars(r, u)
                    dve.wait_ge(part, done + 5)
                    dve.tensor_reduce(flat[:, :, 1, :], trace.rearrange("p j a n -> p j n a"), AX.X,
                                      ALU.add).then_inc(part, 1)
                    for j in range(PAIR):
                        dve.tensor_tensor(mid_v[:, j, :, :], slots[:, j, :, 3:5, :].rearrange("p a b n -> p a (b n)"),
                                          wt[:, j, 128:192].unsqueeze(1).broadcast_to([P, 3, 64]),
                                          ALU.mult).then_inc(part, 1)
                if b:
                    dump_rows(*b)
                if a:
                    dve.wait_ge(part, done + 9)
                    dve.tensor_tensor(mid[:, u % 2, :, 128:160], wt[:, :, 192:224], flat[:, :, 1, :],
                                      ALU.mult).then_inc(part, 1)
                    destinations(r, u)

            def turn_1(a, b):
                ve = outer[:, :, 0:D_VEC].rearrange("p j (a n) -> p j a n", a=3)
                dot = outer[:, :, D_VEC:D_VEC + MUL_V]
                if b:
                    same_targets(*b)
                if a:
                    r, u = a
                    s = RING * r + u
                    done = PARTS * s
                    _, vec, sh, wt, mid_s, mid_v = views(r, u)
                    dve.wait_ge(edges_loaded[u], 32 * r + 32)
                    dve.wait_ge(gathered[u], 32 * r + 32)
                    if not_first(r, u, 1):
                        dve.wait_ge(part, done)
                    dve.tensor_tensor(ve, vec, sh[:, :, 0:3].unsqueeze(3).broadcast_to([P, PAIR, 3, MUL_V]),
                                      ALU.mult).then_inc(part, 1)
                if b:
                    count_before(*b)
                if a:
                    weighted_scalars(r, u)
                    dve.wait_ge(part, done + 1)
                    dve.tensor_reduce(dot, ve.rearrange("p j a n -> p j n a"), AX.X, ALU.add).then_inc(part, 1)
                    for j in range(PAIR):
                        dve.scalar_tensor_tensor(mid_v[:, j, :, 64:96], vec[:, j, :, :], sh[:, j, 3:4],
                                                 wt[:, j, 128:160].unsqueeze(1).broadcast_to([P, 3, MUL_V]),
                                                 ALU.mult, ALU.mult).then_inc(part, 1)
                if b:
                    dump_rows(*b)
                if a:
                    dve.wait_ge(part, done + 5)
                    dve.tensor_tensor(mid_s[:, :, MUL_S:96], wt[:, :, 160:192], dot, ALU.mult).then_inc(part, 1)
                    spread_scalars(r, u)
                    destinations(r, u)

            def turn(r, u):
                a, b = ahead(r, u, 1), ahead(r, u, 2)
                (turn_0 if L0 else turn_1)(a if exists(*a) else None, b if exists(*b) else None)
                if L0 and exists(*ahead(r, u, -1)):
                    add_components(*ahead(r, u, -1))
            with wanted(dve):
                run(dve, turn)


def finish_layer(nc, layer, sem, X, skip, sums, stat, moments, gains, node_vec, acc, out, general, plan):
    groups = TILES // GROUP

    def name(what):
        return sem(f"f{layer}_{what}")

    loaded = [name(f"loaded{g}") for g in range(groups)]
    added, summed, squared, done, roots, ready = (name(k) for k in ("added", "summed", "squared", "done", "roots", "ready"))
    mixed, measured = name("mixed"), name("measured")
    normed_v, normed_a, stored = name("normed_v"), name("normed_a"), name("stored")
    scal, vec = slice(0, MUL_S), slice(MUL_S, D)
    total = sums[:, 0, :, :]
    by_vector = [t for t in range(TILES) if t % 2 == 0]
    by_scalar = [t for t in range(TILES) if t % 2 == 1]

    def wanted(eng):
        return nullcontext() if general is None else eng.If(eng.value_load(general[0:1, 0:1], min_val=0, max_val=1) == 1)

    with nc.Block() as block:
        @block.sync
        def _(sp):
            with wanted(sp):
                for g in range(groups):
                    for c in range(COPIES):
                        sp.dma_start(sums[:, c, GROUP * g:GROUP * (g + 1), :], acc[c][GROUP * g * P:GROUP * (g + 1) * P, :]
                                     .rearrange("(t p) d -> p t d", p=P)).then_inc(loaded[g], 16)
            if layer == 1:
                for g in range(groups):
                    t0, t1 = GROUP * g, min(GROUP * (g + 1), N_NODES // P)
                    sp.wait_ge(normed_v, sum(t < t1 for t in by_vector))
                    sp.wait_ge(normed_a, sum(t < t1 for t in by_scalar))
                    sp.dma_start(out[t0 * P:t1 * P, :].rearrange("(t p) d -> p t d", p=P), X[:, t0:t1, :]).then_inc(stored, 16)
                sp.wait_ge(normed_v, len(by_vector))
                sp.wait_ge(normed_a, len(by_scalar))
                sp.dma_start(out[t1 * P:N_NODES, :], X[0:N_NODES - t1 * P, t1, :]).then_inc(stored, 16)
                sp.wait_ge(stored, 16 * (groups + 1))

        n = [0]

        @block.vector
        def _(dve):
            def step(ins):
                ins.then_inc(done, 1)
                n[0] += 1
                dve.wait_ge(done, n[0])

            with wanted(dve):
                for g in range(groups):
                    ts = slice(GROUP * g, GROUP * (g + 1))
                    dve.wait_ge(loaded[g], 16 * COPIES)
                    for c in range(1, COPIES):
                        dve.tensor_tensor(total[:, ts, :], total[:, ts, :], sums[:, c, ts, :], ALU.add).then_inc(added, 1)
                        dve.wait_ge(added, (COPIES - 1) * g + c)
                    dve.tensor_tensor(skip[:, ts, :], total[:, ts, :], skip[:, ts, :], ALU.add).then_inc(summed, 1)
                dve.wait_ge(summed, groups)
                if layer == 1:
                    for t in range(TILES):
                        residual(dve, t, X, skip, node_vec, mixed)
                    for t in range(TILES):
                        dve.wait_ge(mixed, t + 1)
                        dve.bn_stats(moments[:, t, 0:6], X[:, t, :]).then_inc(measured, 1)
            if layer == 0:
                dve.wait_ge(squared, TILES)
                dve.tensor_scalar(stat[:, 0, :], stat[:, 0, :], 1.0 / MUL_S, EPS, ALU.mult, ALU.add)
                step(dve.tensor_scalar(stat[:, 1, :], stat[:, 1, :], 1.0 / MUL_V, EPS, ALU.mult, ALU.add))
                dve.sem_inc(ready, 1)
                dve.wait_ge(roots, 1)
                step(dve.reciprocal(stat[:, 2:4, :], stat[:, 2:4, :]))
                for t in range(TILES):
                    dve.scalar_tensor_tensor(total[:, t, scal], skip[:, t, scal], stat[:, 2, t:t + 1],
                                             gains[:, 0:MUL_S], ALU.mult, ALU.mult)
                    last = dve.scalar_tensor_tensor(total[:, t, vec].rearrange("p (c n) -> p c n", c=3),
                                                    skip[:, t, vec].rearrange("p (c n) -> p c n", c=3), stat[:, 3, t:t + 1],
                                                    gains[:, MUL_S:].unsqueeze(1).broadcast_to([P, 3, MUL_V]), ALU.mult, ALU.mult)
                step(last)
                dve.tensor_tensor(X[:, :, scal], X[:, :, scal], total[:, :, scal], ALU.add)
                xv = X[:, :, vec].rearrange("p t (n c) -> p t n c", c=3)
                step(dve.tensor_tensor(xv, xv, total[:, :, vec].rearrange("p t (c n) -> p t n c", c=3), ALU.add))
                for t in range(TILES):
                    dve.bn_stats(moments[:, t, 0:6], X[:, t, :]).then_inc(measured, 1)
            dve.wait_ge(measured, TILES)
            for t in range(TILES):
                last = dve.bn_aggr(moments[:, t, 6:8], moments[:, t, 0:6])
            step(last)
            step(dve.tensor_scalar(stat[:, 4, :], moments[:, :, 7], EPS, None, ALU.add))
            dve.sem_inc(ready, 1)
            dve.wait_ge(roots, 2 if layer == 0 else 1)
            step(dve.reciprocal(stat[:, 5, :], stat[:, 5, :]))
            step(dve.scalar_tensor_tensor(stat[:, 4, :], moments[:, :, 6], -1.0, stat[:, 5, :], ALU.mult, ALU.mult))
            dve.sem_inc(ready, 1)
            for t in by_vector:
                dve.tensor_scalar(X[:, t, :], X[:, t, :], moments[:, t, 6:7], stat[:, 5, t:t + 1], ALU.subtract,
                                  ALU.mult).then_inc(normed_v, 1)

        @block.scalar
        def _(act):
            if plan:
                plan["scalar"](act)
            if layer == 0:
                for t in range(TILES):
                    act.wait_ge(summed, t // GROUP + 1)
                    act.activation(sums[:, 1, t, scal], skip[:, t, scal], ACT.Square, accum_out=stat[:, 0, t:t + 1])
                    act.activation(sums[:, 1, t, vec], skip[:, t, vec], ACT.Square,
                                   accum_out=stat[:, 1, t:t + 1]).then_inc(squared, 1)
                act.wait_ge(ready, 1)
                act.activation(stat[:, 2:4, :], stat[:, 0:2, :], ACT.Sqrt).then_inc(roots, 1)
            act.wait_ge(ready, 2 if layer == 0 else 1)
            act.activation(stat[:, 5, :], stat[:, 4, :], ACT.Sqrt).then_inc(roots, 1)
            act.wait_ge(ready, 3 if layer == 0 else 2)
            for t in by_scalar:
                act.activation(X[:, t, :], X[:, t, :], ACT.Identity, bias=stat[:, 4, t:t + 1],
                               scale=stat[:, 5, t:t + 1]).then_inc(normed_a, 1)

        if plan:
            block.gpsimd(plan["pool"])
            block.tensor(plan["tensor"])


WEIGHTS = ["node_s0", "node_v0", "mlp_in0", "mlp_mid0", "mlp_out0", "radial_in1", "out_first0", "out_mid0", "out_last0",
           "node_s1", "node_v1", "mlp_in1", "mlp_out1", "out_s1", "out_v1", "out1_0", "out1_1", "out1_2"]

_F0 = NH0 ** -0.5 * AVG
_F1 = (2.0 / NH1) ** 0.5 * AVG * 0.5 * 96 ** -0.5
SCALES = [
    ("node_s0", 0, MUL_S, MUL_S ** -0.5), ("node_v0", 0, D_VEC, MUL_V ** -0.5),
    ("node_s1", 0, MUL_S, MUL_S ** -0.5), ("node_v1", 0, D_VEC, MUL_V ** -0.5),
    ("out_first0", 0, 64, _F0 * 96 ** -0.5), ("out_first0", 64, 128, _F0 * 128 ** -0.5),
    ("out_last0", 0, 32, _F0 * 96 ** -0.5 * 3 ** -0.5), ("out_last0", 32, 64, _F0 * 128 ** -0.5),
    ("out_last0", 64, 96, _F0 * 128 ** -0.5 * 2 ** -0.5),
    ("out_mid0", 0, 32, _F0 * 128 ** -0.5), ("out_mid0", 32, 64, _F0 * 128 ** -0.5 * 2 ** -0.5),
    ("out_mid0", 64, 96, _F0 * 128 ** -0.5), ("out_mid0", 96, 128, _F0 * 128 ** -0.5 * 2 ** -0.5),
    ("out1_0", 0, 64, _F1), ("out1_0", 64, 96, _F1 * 3 ** -0.5), ("out1_0", 96, 128, _F1),
    ("out1_1", 0, 128, _F1), ("out1_2", 0, 128, _F1),
    ("out_s1", 0, 64, _F1), ("out_s1", 64, 96, _F1 * 3 ** -0.5), ("out_v1", 0, 96, _F1),
]


def kernel(x, src, dst, edge_attr_10, edge_attr_4, edge_attr_8, node_vec1, **p):
    import concourse.bacc as bacc
    from concourse.bass_utils import run_bass_kernel_spmd

    f = np.float32
    x = np.asarray(x)
    a = {k: np.asarray(v) for k, v in p.items()}
    arrays = {}
    arrays["x"] = np.zeros((NODES_PAD, D), f)
    arrays["x"][:N_NODES] = x
    node_vec = np.zeros(NODES_PAD, f)
    node_vec[:N_NODES] = np.asarray(node_vec1)[:, 0]
    arrays["node_vec"] = node_vec.reshape(TILES, P).T
    arrays["gains"] = np.concatenate([a["L0_gnn_g0"], a["L0_gnn_g1"]])
    sh = np.asarray(edge_attr_4)
    arrays["rec"] = np.zeros((EDGES_PAD, REC), f)
    arrays["rec"][:N_EDGES] = np.concatenate([np.asarray(edge_attr_8), np.asarray(edge_attr_10), sh[:, 1:4], sh[:, 0:1]], 1)
    arrays["radial"] = np.ascontiguousarray(arrays["rec"][:, NB0:NB0 + NB1].T)
    arrays["keys"] = np.zeros((EDGES_PAD, 2), np.int32)
    arrays["keys"][:, 1] = NODES_PAD - 1
    arrays["keys"][:N_EDGES, 0] = np.asarray(src)
    arrays["keys"][:N_EDGES, 1] = np.asarray(dst)

    arrays["dst"] = np.ascontiguousarray(arrays["keys"][:, 1])

    def per_component(m):
        b = np.zeros((MUL_V, 3, 3, MUL_V), f)
        for c in range(3):
            b[:, c, c, :] = m
        return b.reshape(D_VEC, D_VEC)

    for n, (s_msg, s_self, v_msg, v_self) in enumerate((("L0_gnn_W1_0", "L0_gnn_Wsc0", "L0_gnn_W1_1", "L0_gnn_Wsc1"),
                                                        ("L1_gnn_W_l1_0", "L1_gnn_W_si0", "L1_gnn_W_l1_1", "L1_gnn_W_si1"))):
        arrays[f"node_s{n}"] = np.concatenate([a[s_msg], a[s_self]], 1)
        arrays[f"node_v{n}"] = np.concatenate([per_component(a[v_msg]), per_component(a[v_self])], 1)
    arrays["mlp_in0"] = np.zeros((PAIR * REC, PAIR * NH0), f)
    arrays["mlp_mid0"] = np.zeros((PAIR * NH0, PAIR * NH0), f)
    arrays["mlp_in1"] = np.zeros((PAIR * REC, PAIR * NH1), f)
    for j in range(PAIR):
        arrays["mlp_in0"][j * REC:j * REC + NB0, j * NH0:(j + 1) * NH0] = a["L0_gnn_Wfc1"]
        arrays["mlp_mid0"][j * NH0:(j + 1) * NH0, j * NH0:(j + 1) * NH0] = a["L0_gnn_Wfc2"]
        arrays["mlp_in1"][j * REC + NB0:j * REC + NB0 + NB1, j * NH1:(j + 1) * NH1] = a["L1_gnn_W_fc1"]
    w3 = a["L0_gnn_Wfc3"]
    w3 = np.concatenate([w3[:, 0:160], w3[:, 192:224], w3[:, 160:192]], 1)
    arrays["mlp_out0"] = np.concatenate([np.pad(w3, ((0, 0), (224 * j, 224 * (PAIR - 1 - j)))) for j in range(PAIR)], 0)
    w3 = a["L1_gnn_W_fc2"]
    arrays["radial_in1"] = a["L1_gnn_W_fc1"]
    arrays["mlp_out1"] = np.concatenate([w3[:, 64:128], w3[:, 0:64], w3[:, 128:192]], 1)
    w_s, w_v = a["L0_gnn_W2_0"], a["L0_gnn_W2_1"]
    arrays["out_first0"] = np.zeros((128, 128), f)
    arrays["out_first0"][64:, 0:MUL_V] = w_v[0:64]
    arrays["out_first0"][0:64, MUL_V:MUL_V + MUL_S] = w_s[0:64]
    arrays["out_last0"] = np.zeros((96, 96), f)
    arrays["out_last0"][0:32, 0:MUL_S] = w_s[64:96]
    arrays["out_last0"][32:, MUL_S:] = w_v[64:]
    arrays["out_mid0"] = np.zeros((128, 64), f)
    arrays["out_mid0"][0:64, 0:MUL_V] = w_v[64:]
    arrays["out_mid0"][64:, MUL_V:] = w_v[64:]
    arrays["out_s1"] = np.concatenate([a["L1_gnn_W_l2_00"], a["L1_gnn_W_l2_10"]], 0)
    arrays["out_v1"] = np.concatenate([a["L1_gnn_W_l2_01"], a["L1_gnn_W_l2_11"]], 0)
    out1 = np.zeros((D_MID, D), f)
    out1[0:96, 0:MUL_S] = arrays["out_s1"]
    for c in range(3):
        out1[96 * (c + 1):96 * (c + 2), MUL_S + c * MUL_V:MUL_S + (c + 1) * MUL_V] = arrays["out_v1"]
    for k in range(D_MID // P):
        arrays[f"out1_{k}"] = out1[k * P:(k + 1) * P]
    arrays = {k: np.ascontiguousarray(v) for k, v in arrays.items()}

    nc = bacc.Bacc("TRN2", target_bir_lowering=False, num_devices=1)
    t_in = {k: nc.dram_tensor("in_" + k, v.shape, mybir.dt.from_np(v.dtype), kind="ExternalInput").ap()
            for k, v in arrays.items()}
    out = nc.dram_tensor("out", (N_NODES, D), F32, kind="ExternalOutput").ap()
    build(nc, t_in, out)
    r = run_bass_kernel_spmd(nc, [{"in_" + k: v for k, v in arrays.items()}], core_ids=[0])
    return r.results[0]["out"]
```
